# Optimizing a Trainium2 kernel written in Bass

```python
import numpy as np
import jax
import jax.numpy as jnp

def _softmax(x, axis=-1):
    return jax.nn.softmax(x, axis=axis)

def _gelu(x):
    return jax.nn.gelu(x, approximate=True)

def _silu(x):
    return jax.nn.silu(x)

def _sigmoid(x):
    return jax.nn.sigmoid(x)

def _layernorm(x, axis=-1, eps=1e-05):
    m = jnp.mean(x, axis=axis, keepdims=True)
    v = jnp.var(x, axis=axis, keepdims=True)
    return (x - m) / jnp.sqrt(v + eps)

def _scatter_add(tgt, idx, src, axis=0):
    return tgt.at[idx].add(src)

def _segment_sum(src, seg, n):
    return jax.ops.segment_sum(src, seg, n)
kernel_name = 'mk_sandwich_d1_jaxref_r4_e3824c'

def setup_inputs(seed: int=0):
    np.random.seed(seed)
    _w = jnp.asarray

    def _L0_attn_setup():
        import jax, jax.numpy as jnp
        import numpy as np
        import math
        D_MODEL = 512
        NUM_HEAD = 16
        HEAD_DIM = D_MODEL // NUM_HEAD

        def _trunc_normal(key, shape, std):
            return jax.random.truncated_normal(key, -3.0, 3.0, shape, dtype=jnp.float32) * std
        key = jax.random.key(seed)
        kx, kp, ko = jax.random.split(key, 3)
        b, s = (4, 512)
        x = jax.random.normal(kx, (b, s, D_MODEL), dtype=jnp.float32)
        sigma_p = math.sqrt(2.0 / (D_MODEL + 3 * D_MODEL))
        w_project = _trunc_normal(kp, (3 * D_MODEL, D_MODEL), sigma_p)
        sigma_o = math.sqrt(2.0 / (D_MODEL + D_MODEL))
        w_out = _trunc_normal(ko, (D_MODEL, D_MODEL), sigma_o)
        return {'x': x, 'w_project': w_project, 'w_out': w_out}
    _L0_attn_in = _L0_attn_setup()

    def _L0_ffn_setup():
        import jax, jax.numpy as jnp
        import numpy as np
        E, K, H, F = (64, 6, 512, 192)
        G, KG = (8, 4)
        SHARED_F = 192
        SCALE = 2.5
        T = 2 * 256
        CAP = 2 * (T * K // E)

        def _grouped_topk(logits, bias):
            scores = jax.nn.sigmoid(logits.astype(jnp.float32))
            scores_b = scores + bias[None, :]
            gs = scores_b.reshape(-1, G, E // G)
            group_scores = jnp.sum(jax.lax.top_k(gs, 2)[0], axis=-1)
            gidx = jax.lax.top_k(group_scores, KG)[1]
            rows = jnp.arange(group_scores.shape[0])[:, None]
            group_mask = jnp.zeros_like(group_scores).at[rows, gidx].set(1.0)
            score_mask = jnp.repeat(group_mask, E // G, axis=-1) > 0
            tmp = jnp.where(score_mask, scores_b, -jnp.inf)
            topk_ids = jax.lax.top_k(tmp, K)[1]
            topk_w = jnp.take_along_axis(scores, topk_ids, axis=-1)
            topk_w = topk_w / jnp.sum(topk_w, axis=-1, keepdims=True)
            return (topk_w * SCALE, topk_ids)

        def _routed_moe(x, topk_w, topk_ids, w_gate, w_up, w_down):
            Tn = x.shape[0]
            flat_e = topk_ids.reshape(-1)
            order = jnp.argsort(flat_e)
            se = flat_e[order]
            pos = jnp.arange(Tn * K) - jnp.searchsorted(se, se, side='left')
            tok = order // K
            valid = pos < CAP
            slot = jnp.where(valid, pos, CAP)
            buf = jnp.zeros((E, CAP + 1, H), x.dtype).at[se, slot].set(x[tok])[:, :CAP]
            h = jax.nn.silu(jnp.einsum('ech,ehf->ecf', buf, w_gate)) * jnp.einsum('ech,ehf->ecf', buf, w_up)
            out = jnp.einsum('ecf,efh->ech', h, w_down)
            gathered = out[se, jnp.minimum(pos, CAP - 1)] * valid.astype(x.dtype)[:, None]
            w = topk_w.reshape(-1)[order].astype(x.dtype)[:, None]
            return jax.ops.segment_sum(gathered * w, tok, num_segments=Tn)
        key = jax.random.key(seed)
        ks = jax.random.split(key, 9)
        s = 0.02
        return dict(hidden_states=jax.random.normal(ks[0], (2, 256, H), jnp.float32), gate_w=jax.random.normal(ks[1], (H, E), jnp.float32) * s, bias=jax.random.normal(ks[2], (E,), jnp.float32) * s, w_gate=jax.random.normal(ks[3], (E, H, F), jnp.float32) * s, w_up=jax.random.normal(ks[4], (E, H, F), jnp.float32) * s, w_down=jax.random.normal(ks[5], (E, F, H), jnp.float32) * s, ws_gate=jax.random.normal(ks[6], (H, SHARED_F), jnp.float32) * s, ws_up=jax.random.normal(ks[7], (H, SHARED_F), jnp.float32) * s, ws_down=jax.random.normal(ks[8], (SHARED_F, H), jnp.float32) * s)
    _L0_ffn_in = _L0_ffn_setup()
    _d = {'L0_attn_x': _L0_attn_in['x'], 'L0_attn_w_project': _L0_attn_in['w_project'], 'L0_attn_w_out': _L0_attn_in['w_out'], 'L0_ffn_gate_w': _L0_ffn_in['gate_w'], 'L0_ffn_bias': _L0_ffn_in['bias'], 'L0_ffn_w_gate': _L0_ffn_in['w_gate'], 'L0_ffn_w_up': _L0_ffn_in['w_up'], 'L0_ffn_w_down': _L0_ffn_in['w_down'], 'L0_ffn_ws_gate': _L0_ffn_in['ws_gate'], 'L0_ffn_ws_up': _L0_ffn_in['ws_up'], 'L0_ffn_ws_down': _L0_ffn_in['ws_down']}
    _x0 = _d['L0_attn_x']
    _d['L0_attn_x'] = jax.random.normal(jax.random.fold_in(jax.random.key(seed), 1), (8, 1024, 512), dtype=_x0.dtype)
    del _x0
    return _d

def reference(L0_attn_x, L0_attn_w_project, L0_attn_w_out, L0_ffn_gate_w, L0_ffn_bias, L0_ffn_w_gate, L0_ffn_w_up, L0_ffn_w_down, L0_ffn_ws_gate, L0_ffn_ws_up, L0_ffn_ws_down):

    def _L0_attn_ref(x, w_project, w_out):
        import jax, jax.numpy as jnp
        import numpy as np
        import math
        D_MODEL = 512
        NUM_HEAD = 16
        HEAD_DIM = D_MODEL // NUM_HEAD

        def _trunc_normal(key, shape, std):
            return jax.random.truncated_normal(key, -3.0, 3.0, shape, dtype=jnp.float32) * std
        b, s, d = x.shape
        qkv = jnp.einsum('bsd,od->bso', x, w_project)
        qkv = qkv.reshape(b, s, 3, NUM_HEAD, HEAD_DIM)
        qkv = jnp.transpose(qkv, (2, 0, 3, 1, 4))
        q, k, v = (qkv[0], qkv[1], qkv[2])
        att = jnp.einsum('bhqd,bhkd->bhqk', q, k) / math.sqrt(HEAD_DIM)
        causal = jnp.triu(jnp.ones((s, s), dtype=bool), k=1)
        att = jnp.where(causal[None, None, :, :], jnp.float32(-1000000000.0), att)
        att = jax.nn.softmax(att, axis=-1)
        out = jnp.einsum('bhqk,bhkd->bhqd', att, v)
        out = jnp.transpose(out, (0, 2, 1, 3)).reshape(b, s, d)
        return jnp.einsum('bsd,od->bso', out, w_out)

    def _L0_ffn_ref(hidden_states, gate_w, bias, w_gate, w_up, w_down, ws_gate, ws_up, ws_down):
        import jax, jax.numpy as jnp
        import numpy as np
        E, K, H, F = (64, 6, 512, 192)
        G, KG = (8, 4)
        SHARED_F = 192
        SCALE = 2.5
        T = 2 * 256
        CAP = 2 * (T * K // E)

        def _grouped_topk(logits, bias):
            scores = jax.nn.sigmoid(logits.astype(jnp.float32))
            scores_b = scores + bias[None, :]
            gs = scores_b.reshape(-1, G, E // G)
            group_scores = jnp.sum(jax.lax.top_k(gs, 2)[0], axis=-1)
            gidx = jax.lax.top_k(group_scores, KG)[1]
            rows = jnp.arange(group_scores.shape[0])[:, None]
            group_mask = jnp.zeros_like(group_scores).at[rows, gidx].set(1.0)
            score_mask = jnp.repeat(group_mask, E // G, axis=-1) > 0
            tmp = jnp.where(score_mask, scores_b, -jnp.inf)
            topk_ids = jax.lax.top_k(tmp, K)[1]
            topk_w = jnp.take_along_axis(scores, topk_ids, axis=-1)
            topk_w = topk_w / jnp.sum(topk_w, axis=-1, keepdims=True)
            return (topk_w * SCALE, topk_ids)

        def _routed_moe(x, topk_w, topk_ids, w_gate, w_up, w_down):
            Tn = x.shape[0]
            flat_e = topk_ids.reshape(-1)
            order = jnp.argsort(flat_e)
            se = flat_e[order]
            pos = jnp.arange(Tn * K) - jnp.searchsorted(se, se, side='left')
            tok = order // K
            valid = pos < CAP
            slot = jnp.where(valid, pos, CAP)
            buf = jnp.zeros((E, CAP + 1, H), x.dtype).at[se, slot].set(x[tok])[:, :CAP]
            h = jax.nn.silu(jnp.einsum('ech,ehf->ecf', buf, w_gate)) * jnp.einsum('ech,ehf->ecf', buf, w_up)
            out = jnp.einsum('ecf,efh->ech', h, w_down)
            gathered = out[se, jnp.minimum(pos, CAP - 1)] * valid.astype(x.dtype)[:, None]
            w = topk_w.reshape(-1)[order].astype(x.dtype)[:, None]
            return jax.ops.segment_sum(gathered * w, tok, num_segments=Tn)
        orig_shape = hidden_states.shape
        x = hidden_states.reshape(-1, H)
        router_logits = x @ gate_w
        topk_w, topk_ids = _grouped_topk(router_logits, bias)
        y = _routed_moe(x, topk_w, topk_ids, w_gate, w_up, w_down)
        shared = jax.nn.silu(x @ ws_gate) * (x @ ws_up) @ ws_down
        return (y + shared).reshape(orig_shape)
    x = L0_attn_x
    x = x + _layernorm(_L0_attn_ref(_layernorm(x, axis=-1), L0_attn_w_project, L0_attn_w_out), axis=-1)
    x = x + _layernorm(_L0_ffn_ref(_layernorm(x, axis=-1), L0_ffn_gate_w, L0_ffn_bias, L0_ffn_w_gate, L0_ffn_w_up, L0_ffn_w_down, L0_ffn_ws_gate, L0_ffn_ws_up, L0_ffn_ws_down), axis=-1)
    return x

_drawn_inputs = setup_inputs


def setup_inputs(seed=0):
    import zlib

    import numpy as np

    out = dict(_drawn_inputs(seed))
    spreads = {}
    factors = {}
    for name, (base, spread) in spreads.items():
        noise = np.random.default_rng([zlib.crc32(name.encode()), seed]).standard_normal(out[name].shape)
        drawn = base * np.exp(spread * noise) if base else spread * noise
        out[name] = jnp.asarray(drawn.astype(out[name].dtype))
    for name, factor in factors.items():
        out[name] = (out[name] * factor).astype(out[name].dtype)
    return out
```

```python
from contextlib import ExitStack

import concourse.bass as bass
from concourse import mybir

P = 128
F32 = mybir.dt.float32
F16 = mybir.dt.float16
BF16 = mybir.dt.bfloat16
U32 = mybir.dt.uint32
ALU = mybir.AluOpType
ACT = mybir.ActivationFunctionType
AX_X = mybir.AxisListType.X

S_X = 16.0
S_W = 64.0
S_QK = 4.0
S_V = 16.0
S_P = 1024.0
S_H = 64.0
M_HI = 4096.0
BIG = 1.0e30
NO_SLOT = 1.0e6


def sandwich_kernel(nc, x, w_qkv_t, w_out_t, gate_w, bias, w_gate, w_up, w_down, ws_gate, ws_up, ws_down, out):
    NB, SEQ, D = x.shape
    NT = SEQ // P
    C = D // P
    NH = 16
    DH = D // NH
    E = gate_w.shape[1]
    FF = w_gate.shape[2]
    FR = FF - P
    K = 6
    G, KG = 8, 4
    ROUTE_SCALE = 2.5
    CAP = 2 * (512 * K // E)
    TOK = NB * SEQ
    XW = D + E
    HPC = P // DH
    EPS = 1e-5
    FW = 2 * FF + E
    VC = 2 * DH + 2
    HALF = SEQ // 2
    HT = HALF // P
    SM_SCALE = float(DH) ** -0.5 / (S_QK * S_QK)
    LN_SP = 6.931471805599453

    GROUPS = []
    for half in range(2):
        for j in range(0, (half + 1) * HT, 2):
            GROUPS.append((half, [(jj, max(jj, half * HT)) for jj in (j, j + 1)]))
    NG = len(GROUPS)

    def group_blocks(g):
        half, blocks = GROUPS[g]
        res, col = [], 0
        for j, i0 in blocks:
            w = ((half + 1) * HT - i0) * P
            if col // 512 != (col + w - 1) // 512:
                col = (col + 511) // 512 * 512
            res.append((j, i0, w, col))
            col += w
        return res, col

    xw_d = nc.dram_tensor("xw_rows", (TOK + P, XW), F32, kind="Internal").ap()
    x1_d = nc.dram_tensor("x_after_attention", (TOK, D), F32, kind="Internal").ap()
    y_d = nc.dram_tensor("ffn_rows", (TOK + P, D), F32, kind="Internal").ap()
    slot_d = nc.dram_tensor("token_of_slot", (CAP * E, 1), U32, kind="Internal").ap()

    outf = out.rearrange("b s d -> (b s) d")
    xf = x.rearrange("b s d -> (b s) d")

    with ExitStack() as ctx:
        def sb(name, cols, dt=F32, parts=P):
            return ctx.enter_context(nc.sbuf_tensor(name, [parts, cols], dt))

        def sem(name):
            return ctx.enter_context(nc.semaphore(name))

        def view(region, off, cols, dt=F32):
            words = cols * (4 if dt in (F32, U32) else 2) // 4
            ap = region[:, off:off + words]
            return ap if dt == F32 else ap.bitcast(dt)

        wqkv = sb("wqkv", 2 * C * 3 * D, F16)[:, :].rearrange("p (l c o) -> p l c o", l=2, c=C)
        wo = sb("wo", 2 * C * D, F16)[:, :].rearrange("p (l c o) -> p l c o", l=2, c=C)
        wff = sb("wff", 2 * C * FW, F16)[:, :].rearrange("p (l c o) -> p l c o", l=2, c=C)
        wdn = sb("wdn", 2 * 2 * D, F16)[:, :].rearrange("p (l c o) -> p l c o", l=2, c=2)
        ident = sb("ident", P)
        ident_b = sb("ident_b", P, BF16)
        mask_qk = sb("mask_qk", P, BF16)
        mask_kq = sb("mask_kq", P, BF16)
        earlier = sb("earlier", P, BF16)
        ones_b = sb("ones_b", P, BF16)
        zeros_row = sb("zeros_row", XW)
        bias_b = sb("bias_b", E)
        slot_e = sb("slot_e", E)
        mhalf = sb("mhalf", NT)
        ln_sp = sb("ln_sp", 1)
        xr_reg = sb("xr_reg", NT * D)
        xr = xr_reg[:, :].rearrange("p (t d) -> p t d", t=NT)
        xt_reg = sb("xt_reg", C * SEQ)
        xT = xt_reg[:, :].bitcast(F16).rearrange("p (l c s) -> p l c s", l=2, c=C)
        o_sb = xt_reg[:, :].rearrange("p (t d) -> p t d", t=NT)
        stack = sb("stack", NH * SEQ)
        stq = view(stack, 0, NH * SEQ, F16).rearrange("p (h s) -> p h s", h=NH)
        stk = view(stack, NH * SEQ // 2, NH * SEQ, F16).rearrange("p (h s) -> p h s", h=NH)
        stage = sb("stage", 2 * 2 * SEQ)
        stg = stage[:, :].bitcast(F16).rearrange("p (n l c s) -> p n l c s", n=2, l=2, c=2)
        v_reg = sb("v_reg", NT * NH * VC // 2)
        vv = v_reg[:, :].bitcast(F16).rearrange("p (t h c) -> p t h c", t=NT, h=NH)
        pt = sb("pt", 2 * 1024 + 3 * 1024)
        p32 = view(pt, 0, 2048).rearrange("p (n c) -> p n c", n=2)
        phl = view(pt, 2048, 3 * 2048, F16).rearrange("p (n l c) -> p n l c", n=3, l=2)
        xn = sb("xn", 2 * D)[:, :].rearrange("p (n d) -> p n d", n=2)
        mx = sb("mx", NH * NT)
        mrow = sb("mrow", 2 * P, F16)[:, :].rearrange("p (l q) -> p l q", l=2)
        olo = sb("olo", 2 * HT * DH)[:, :].rearrange("p (n i d) -> p n i d", n=2, i=HT)
        osum = sb("osum", HT * DH)[:, :].rearrange("p (i d) -> p i d", i=HT)
        orec = sb("orec", HT)[:, :].rearrange("p (i o) -> p i o", o=1)
        stats = sb("stats", NT * 6)[:, :].rearrange("p (t s) -> p t s", t=NT)
        mv = sb("mv", NT * 2)[:, :].rearrange("p (t s) -> p t s", t=NT)
        ve = sb("ve", NT)
        rstd = sb("rstd", NT)
        st2 = sb("st2", 4 * 6)[:, :].rearrange("p (n s) -> p n s", n=4)
        mv2 = sb("mv2", 4 * 2)[:, :].rearrange("p (n s) -> p n s", n=4)
        ve2 = sb("ve2", 4)
        rs2 = sb("rs2", 4)
        oT = view(pt, 0, 2 * 2 * D, F16).rearrange("p (n l s) -> p n l s", n=2, l=2)
        x2T = view(pt, 1024, 2 * 2 * D, F16).rearrange("p (n l s) -> p n l s", n=2, l=2)
        gex = view(pt, 2048, FF + E)
        grc = view(pt, 2304, FF)
        hid = view(pt, 2496, FF)
        hT = view(pt, 2688, 2 * 2 * P, F16).rearrange("p (l c s) -> p l c s", l=2, c=2)
        ysh = view(pt, 2944, 2 * D).rearrange("p (n d) -> p n d", n=2)
        def rt(k, n=NT * E):
            return view(stage, k * NT * E, n)
        sc = rt(0).rearrange("p (t e) -> p t e", t=NT)
        scb = rt(1).rearrange("p (t e) -> p t e", t=NT)
        cand = rt(2).rearrange("p (t e) -> p t e", t=NT)
        rest = rt(3).rearrange("p (t e) -> p t e", t=NT)
        sel = rt(4).rearrange("p (t e) -> p t e", t=NT)
        wgt = rt(5).rearrange("p (t e) -> p t e", t=NT)
        neg = rt(6).rearrange("p (t e) -> p t e", t=NT)
        sel_b = view(stage, 7 * NT * E, NT * E, BF16).rearrange("p (t e) -> p t e", t=NT)
        before_b = view(stage, 7 * NT * E + NT * E // 2, NT * E, BF16).rearrange("p (t e) -> p t e", t=NT)
        gpad = sb("gpad", NT * 2 * G)[:, :].rearrange("p (t g) -> p t g", t=NT)
        gout = sb("gout", NT * 2 * G)[:, :].rearrange("p (t g) -> p t g", t=NT)
        top8 = sb("top8", NT * 8)[:, :].rearrange("p (t g) -> p t g", t=NT)
        gmask = sb("gmask", NT * G)
        gneg = sb("gneg", NT * G)
        wsum = sb("wsum", NT)[:, :].rearrange("p (t o) -> p t o", o=1)
        carry = sb("carry", E)
        slot_i = sb("slot_i", NT * 8, U32)[:, :].rearrange("p (t k) -> p t k", t=NT)
        tok_f = sb("tok_f", NT)
        tok_i = sb("tok_i", NT, U32)

        PS = ctx.enter_context(nc.psum_tensor("PS", [P, 8 * 512], F32))

        def bank(n, cols=512, first=0):
            return PS[:, n * 512 + first:n * 512 + first + cols]

        def o_bank(half):
            return bank(4 + half, HT * (2 * DH + 1)).rearrange("p (i c) -> p i c", i=HT)

        held = {e: sem(f"held_{e}") for e in ("sp", "pool", "dve")}

        def hold(name, eng, s, value):
            eng.wait_ge(s, value)
            eng.sem_inc(held[name], 1)

        s_const = sem("s_const")
        s_vconst = sem("s_vconst")
        s_wld = sem("s_wld")
        s_whi = sem("s_whi")
        s_wlo = sem("s_wlo")
        s_init = sem("s_init")
        x_in = [sem("x_in0"), sem("x_in1")]
        ln_stat = sem("ln_stat")
        ln_eps = sem("ln_eps")
        ln_rstd = sem("ln_rstd")
        xn_ready = sem("xn_ready")
        xt_psum = sem("xt_psum")
        xt_hi = sem("xt_hi")
        xt_lo = sem("xt_lo")
        qkv_psum = sem("qkv_psum")
        qkv_hi = sem("qkv_hi")
        qkv_lo = sem("qkv_lo")
        stacked = [sem("stacked0"), sem("stacked1")]
        s_psum = sem("s_psum")
        max_done = sem("max_done")
        mt_psum = sem("mt_psum")
        m_hi = sem("m_hi")
        m_lo = sem("m_lo")
        m_rows = sem("m_rows")
        st_psum = sem("st_psum")
        exp_done = sem("exp_done")
        ph_act = sem("ph_act")
        ph_dve = sem("ph_dve")
        pl_done = sem("pl_done")
        pv_done = sem("pv_done")
        olo_done = sem("olo_done")
        o_step = sem("o_step")
        o_done = sem("o_done")
        to_psum = sem("to_psum")
        ot_hi = sem("ot_hi")
        ot_lo = sem("ot_lo")
        a_psum = sem("a_psum")
        statv = sem("statv")
        pow_in = sem("pow_in")
        pow_out = sem("pow_out")
        x1_step = sem("x1_step")
        x1_ready = sem("x1_ready")
        xn2_ready = sem("xn2_ready")
        xn_out = [sem("xn_out0"), sem("xn_out1")]
        x1_out = sem("x1_out")
        tx_psum = sem("tx_psum")
        x2_hi = sem("x2_hi")
        x2_lo = sem("x2_lo")
        ff_psum = sem("ff_psum")
        ff_exp = sem("ff_exp")
        h_step = sem("h_step")
        h_ready = sem("h_ready")
        th_psum = sem("th_psum")
        ht_hi = sem("ht_hi")
        ht_lo = sem("ht_lo")
        dn_psum = sem("dn_psum")
        y_sb = sem("y_sb")
        y_out = [sem("y_out0"), sem("y_out1")]
        r_step = sem("r_step")
        r_carry = sem("r_carry")
        sel_ready = sem("sel_ready")
        pos_psum = sem("pos_psum")
        wgt_ready = sem("wgt_ready")
        wgt_out = sem("wgt_out")
        slot_ready = sem("slot_ready")
        tok_ready = sem("tok_ready")
        slot_put = sem("slot_put")

        R = 4
        wup = view(stack, 0, R * 2 * C * FF).rearrange("p (n k c f) -> p n k c f", n=R, k=2, c=C)
        wdo = view(stack, R * 2 * C * FF, R * 2 * D).rearrange("p (n k d) -> p n k d", n=R, k=2)
        xg = view(xt_reg, 0, R * XW).rearrange("p (n d) -> p n d", n=R)
        xgT = view(xt_reg, R * XW, 2 * C * CAP).rearrange("p (n c s) -> p n c s", n=2, c=C)
        exg = view(xt_reg, R * XW + 2 * C * CAP, 2 * CAP).rearrange("p (k s) -> p k s", k=2)
        exh = view(xt_reg, R * XW + 2 * C * CAP + 2 * CAP, 2 * 2 * CAP).rearrange("p (n k s) -> p n k s", n=2, k=2)
        oe = view(xr_reg, 0, 2 * D).rearrange("p (n d) -> p n d", n=2)
        slots = view(xr_reg, 2 * D, E, U32)
        slot_c = view(xr_reg, 2 * D + E, R, U32)
        idx_in = sem("idx_in")
        w_in = [sem(f"w_in{n}") for n in range(R)]
        idx_c = sem("idx_c")
        xg_in = [sem(f"xg_in{n}") for n in range(R)]
        xgt_psum = sem("xgt_psum")
        xgt_sb = sem("xgt_sb")
        up_psum = sem("up_psum")
        e_exp = sem("e_exp")
        e_step = sem("e_step")
        e_hid = sem("e_hid")
        eo_psum = sem("eo_psum")
        oe_ready = sem("oe_ready")
        oe_free = sem("oe_free")
        added = sem("added")
        all_added = sem("all_added")
        FT = 4
        fy = view(stack, 0, 2 * FT * D).rearrange("p (n t d) -> p n t d", n=2, t=FT)
        fx = view(stack, 2 * FT * D, 2 * FT * D).rearrange("p (n t d) -> p n t d", n=2, t=FT)
        f_st = sb("f_st", 2 * FT * 6)[:, :].rearrange("p (n t s) -> p n t s", n=2, t=FT)
        f_mv = sb("f_mv", 2 * FT * 2)[:, :].rearrange("p (n t s) -> p n t s", n=2, t=FT)
        f_ve = sb("f_ve", 2 * FT)[:, :].rearrange("p (n t) -> p n t", n=2)
        f_rs = sb("f_rs", 2 * FT)[:, :].rearrange("p (n t) -> p n t", n=2)
        f_in = [sem("f_in0"), sem("f_in1")]
        f_stat = sem("f_stat")
        f_var = sem("f_var")
        f_eps = sem("f_eps")
        f_rstd = sem("f_rstd")
        f_norm = sem("f_norm")
        f_sum = sem("f_sum")
        f_out = [sem("f_out0"), sem("f_out1")]
        NF = TOK // (FT * P)

        def experts_sync(sp):
            sp.wait_ge(slot_put, NB * 16 * NT * K)
            sp.dma_start(slots[0:CAP, :], slot_d.rearrange("(s e) o -> s (e o)", e=E)).then_inc(idx_in, 16)
            with sp.Fori(0, E // R) as e0_turn:
                e0 = e0_turn * R
                for n in range(R):
                    sp.wait_ge(eo_psum, e0 + n + 1)
                    ups = lambda w: w[bass.ds(e0 + n, 1), :, :].rearrange("o (p c) f -> (o p) c f", c=C)
                    sp.dma_start(wup[:, n, 0, :, :], ups(w_gate)).then_inc(w_in[n], 16)
                    sp.dma_start(wup[:, n, 1, :, :], ups(w_up)).then_inc(w_in[n], 16)
                    down = w_down[bass.ds(e0 + n, 1), :, :].rearrange("o f d -> (o f) d")
                    sp.dma_start(wdo[:, n, 0, :], down[0:P, :]).then_inc(w_in[n], 16)
                    sp.dma_start(wdo[0:FR, n, 1, :], down[P:FF, :]).then_inc(w_in[n], 16)
            sp.wait_ge(all_added, 1)

            def final(i, n):
                rows = lambda d: d[bass.ds(i * (FT * P) + n * (FT * P), FT * P), :].rearrange("(t p) d -> p t d", p=P)
                sp.dma_start(fy[:, n, :, :], rows(y_d)).then_inc(f_in[n], 16)
                sp.dma_start(fx[:, n, :, :], rows(x1_d)).then_inc(f_in[n], 16)

            def store(i, n):
                sp.wait_ge(f_sum, i + n + 1)
                dst = outf[bass.ds(i * (FT * P) + n * (FT * P), FT * P), :].rearrange("(t p) d -> p t d", p=P)
                sp.dma_start(dst, fy[:, n, :, :]).then_inc(f_out[n], 16)

            final(0, 0)
            final(0, 1)
            with sp.Fori(0, (NF - 2) // 2) as i_turn:
                i = i_turn * 2
                for n in range(2):
                    store(i, n)
                    sp.wait_ge(f_out[n], i * 8 + 16)
                    final(i + 2, n)
            for n in range(2):
                store(NF - 2, n)
            for n in range(2):
                sp.wait_ge(f_out[n], 16 * NF // 2)

        def experts_pool(pool):
            g = nc.gpsimd

            def gather(e, n):
                g.tensor_copy(slot_c[0:CAP, n:n + 1], slots[0:CAP, bass.ds(e, 1)]).then_inc(idx_c, 1)
                hold("pool", pool, idx_c, e + 1)
                g.indirect_dma_start(out=xg[0:CAP, n, :], out_offset=None, in_=xw_d,
                                     in_offset=bass.IndirectOffsetOnAxis(ap=slot_c[0:CAP, n:n + 1], axis=0),
                                     bounds_check=TOK + P - 1, oob_is_err=True).then_inc(xg_in[n], 16)

            def add(e, n):
                hold("pool", pool, oe_ready, e + 1)
                g.indirect_dma_start(out=y_d, out_offset=bass.IndirectOffsetOnAxis(ap=slot_c[0:CAP, n:n + 1], axis=0),
                                     in_=oe[0:CAP, n % 2, :], in_offset=None, bounds_check=TOK + P - 1,
                                     oob_is_err=True, compute_op=ALU.add).then_inc(added, 16)
                hold("pool", pool, added, e * 16 + 16)
                pool.sem_inc(oe_free, 1)

            hold("pool", pool, idx_in, 16)
            for n in range(2):
                hold("pool", pool, xn_out[n], NB * NT * 8)
                hold("pool", pool, y_out[n], NB * NT * 8)
            hold("pool", pool, wgt_out, NB * 16)
            hold("pool", pool, eo_psum, R)
            gather(0, 0)
            gather(1, 1)
            with pool.Fori(0, (E - R) // R) as e0_turn:
                e0 = e0_turn * R
                for n in range(R):
                    gather(e0 + n + 2, (n + 2) % R)
                    add(e0 + n, n)
            for n in range(R):
                if n + 2 < R:
                    gather(E - R + n + 2, n + 2)
                add(E - R + n, n)
            pool.sem_inc(all_added, 1)
            with pool.Fori(0, NF // 2) as i_turn:
                i = i_turn * 2
                for n in range(2):
                    hold("pool", pool, f_var, i + n + 1)
                    g.tensor_scalar(f_ve[:, n, :], f_mv[:, n, :, 1], EPS, None, ALU.add).then_inc(f_eps, 1)
                    hold("pool", pool, f_eps, i + n + 1)
                    g.tensor_tensor(f_rs[:, n, :], f_ve[:, n, :], mhalf[:, 0:FT], ALU.pow).then_inc(f_rstd, 1)

        def experts_act(act):
            a = nc.scalar
            with act.Fori(0, E // 2) as e0_turn:
                e0 = e0_turn * 2
                for n in range(2):
                    act.wait_ge(xgt_psum, e0 + n + 1)
                    a.activation(xgT[:, n, :, :], bank(n, C * CAP).rearrange("p (c s) -> p c s", c=C),
                                 ACT.Copy).then_inc(xgt_sb, 1)
                    act.wait_ge(up_psum, e0 + n + 1)
                    act.wait_ge(e_hid, e0 + n + 1)
                    a.activation(exg[:, 0, :], bank(2 + n, CAP), ACT.Exp, scale=-1.0).then_inc(e_exp, 1)
                    a.activation(exg[0:FR, 1, :], bank(2 + n, CAP, CAP)[0:FR], ACT.Exp, scale=-1.0).then_inc(e_exp, 1)

        def experts_dve(dve):
            v = nc.vector
            dve.sem_inc(e_hid, 1)
            with dve.Fori(0, E // R) as e0_turn:
                e0 = e0_turn * R
                for n in range(R):
                    m = n % 2
                    dve.wait_ge(e_exp, (e0 + n) * 2 + 2)
                    blocks = [(0, P), (1, FR)]
                    k = (e0 + n) * 6
                    for i, (j, kp) in enumerate(blocks):
                        v.tensor_scalar(exg[0:kp, j, :], exg[0:kp, j, :], 1.0, None, ALU.add).then_inc(e_step, 1)
                    for i, (j, kp) in enumerate(blocks):
                        dve.wait_ge(e_step, k + i + 1)
                        v.reciprocal(exg[0:kp, j, :], exg[0:kp, j, :]).then_inc(e_step, 1)
                    for i, (j, kp) in enumerate(blocks):
                        dve.wait_ge(e_step, k + i + 3)
                        v.tensor_tensor(exh[0:kp, m, j, :], bank(2 + m, CAP, j * CAP)[0:kp], exg[0:kp, j, :],
                                        ALU.mult).then_inc(e_step, 1)
                    for i, (j, kp) in enumerate(blocks):
                        dve.wait_ge(e_step, k + i + 5)
                        ins = v.tensor_tensor(exh[0:kp, m, j, :], bank(2 + m, CAP, (2 + j) * CAP)[0:kp],
                                              exh[0:kp, m, j, :], ALU.mult)
                    ins.then_inc(e_hid, 1)
                    weigh(dve, e0 + n, n)

            with dve.Fori(0, NF // 2) as i_turn:
                i = i_turn * 2
                for n in range(2):
                    dve.wait_ge(f_in[n], i * 16 + 32)
                    for t in range(FT):
                        ins = v.bn_stats(f_st[:, n, t, :], fy[:, n, t, :])
                    ins.then_inc(f_stat, 1)
                    hold("dve", dve, f_stat, i + n + 1)
                    for t in range(FT):
                        ins = v.bn_aggr(f_mv[:, n, t, :], f_st[:, n, t, :])
                    ins.then_inc(f_var, 1)
                for n in range(2):
                    dve.wait_ge(f_rstd, i + n + 1)
                    for t in range(FT):
                        ins = v.tensor_scalar(fy[:, n, t, :], fy[:, n, t, :], f_mv[:, n, t, 0:1], f_rs[:, n, t:t + 1],
                                              ALU.subtract, ALU.mult)
                    ins.then_inc(f_norm, 1)
                    dve.wait_ge(f_norm, i + n + 1)
                    v.tensor_tensor(fy[:, n, :, :], fy[:, n, :, :], fx[:, n, :, :], ALU.add).then_inc(f_sum, 1)

        def weigh(dve, e, n):
            dve.wait_ge(eo_psum, R + e + 1)
            dve.wait_ge(oe_free, e + 1)
            nc.vector.tensor_scalar(oe[0:CAP, n % 2, :], bank(4 + n % 2)[0:CAP], xg[0:CAP, n, bass.ds(D + e, 1)], None,
                                    ALU.mult).then_inc(oe_ready, 1)

        def experts_pe(pe):
            mm = nc.tensor.matmul
            pe.drain().then_inc(eo_psum, R)

            def turn(e, n, round_):
                pe.wait_ge(xg_in[n], round_)
                for c in range(C):
                    ins = nc.tensor.transpose(bank(n % 2, CAP, c * CAP), xg[0:CAP, n, c:D:C], ident[0:CAP, 0:CAP])
                ins.then_inc(xgt_psum, 1)

            def up(e, n, round_):
                pe.wait_ge(xgt_sb, e + 1)
                pe.wait_ge(w_in[n], round_)
                for k in range(2):
                    for j, kp in ((0, P), (1, FR)):
                        for c in range(C):
                            ins = mm(bank(2 + n % 2, CAP, (2 * k + j) * CAP)[0:kp], wup[:, n, k, c, j * P:j * P + kp],
                                     xgT[:, n % 2, c, :], start=c == 0, stop=c == C - 1)
                ins.then_inc(up_psum, 1)

            def down(e, n):
                pe.wait_ge(e_hid, e + 2)
                mm(bank(4 + n % 2)[0:CAP], exh[:, n % 2, 0, :], wdo[:, n, 0, :], start=True, stop=False)
                mm(bank(4 + n % 2)[0:CAP], exh[0:FR, n % 2, 1, :], wdo[0:FR, n, 1, :], start=False,
                   stop=True).then_inc(eo_psum, 1)

            def steady(j, i, q):
                turn(j + 2, (i + 2) % R, q * 4 + (16 if i + 2 < R else 32))
                up(j + 1, (i + 1) % R, q * 16 + (64 if i + 1 < R else 128))
                down(j, i)

            turn(0, 0, 16)
            turn(1, 1, 16)
            up(0, 0, 64)
            with pe.Fori(0, (E - R) // R) as e0_turn:
                e0 = e0_turn * R
                for i in range(R):
                    steady(e0 + i, i, e0)
            for i in range(R - 2):
                steady(E - R + i, i, E - R)
            up(E - 1, R - 1, (E // R) * 64)
            down(E - 2, R - 2)
            down(E - 1, R - 1)

        slot_init = sb("slot_init", E, U32)
        cols_i = sb("cols_i", E, U32)
        N_CONST = 16

        block = ctx.enter_context(nc.Block())

        w32 = view(stack, 0, C * 3 * D).rearrange("p (c o) -> p c o", c=C)
        wo32 = view(stack, C * 3 * D, C * D).rearrange("p (c o) -> p c o", c=C)
        wff32 = view(stack, C * 4 * D, C * FW).rearrange("p (c o) -> p c o", c=C)
        wdn32 = view(stack, C * 4 * D + C * FW, 2 * D).rearrange("p (c o) -> p c o", c=2)
        SPLITS = [(w32, wqkv, P), (wo32, wo, P), (wff32, wff, P),
                  (wdn32[:, 0, :], wdn[:, :, 0, :], P), (wdn32[0:FR, 1, :], wdn[0:FR, :, 1, :], FR)]

        X1S = NT + 3 * NT
        HS = 4 * NT
        RS = 66
        ph_by_dve = [g in (2, 3) for g in range(NG)]
        n_ph_dve = sum(ph_by_dve)
        n_ph_act = NG - n_ph_dve

        @block.sync
        def _(sp):
            ld = lambda d, s: sp.dma_start(d, s).then_inc(s_wld, 16)
            ld(w32, w_qkv_t.rearrange("(c p) o -> p c o", p=P))
            ld(wo32, w_out_t.rearrange("(c p) o -> p c o", p=P))
            ld(wff32[:, :, 0:FF], ws_gate.rearrange("(c p) o -> p c o", p=P))
            ld(wff32[:, :, FF:FF + E], gate_w.rearrange("(c p) o -> p c o", p=P))
            ld(wff32[:, :, FF + E:FW], ws_up.rearrange("(c p) o -> p c o", p=P))
            ld(wdn32[:, 0, :], ws_down[0:P, :])
            ld(wdn32[0:FR, 1, :], ws_down[P:FF, :])
            ld(bias_b[:, :], bias.partition_broadcast(P))
            sp.wait_ge(s_const, N_CONST)
            sp.dma_start(xw_d[TOK:TOK + P, :], zeros_row[:, :]).then_inc(s_init, 16)
            sp.dma_start(y_d[TOK:TOK + P, :], zeros_row[:, 0:D]).then_inc(x1_out, 16)
            sp.dma_start(slot_d.rearrange("(s e) o -> s (e o)", e=E), slot_init[0:CAP, :]).then_inc(s_init, 16)
            with sp.Fori(0, NB) as b:
                sp.wait_ge(x1_out, b * (16 * NT) + 16)
                for n in range(2):
                    src = xf[bass.ds(b * SEQ + n * HALF, HALF), :].rearrange("(t p) d -> p t d", p=P)
                    sp.dma_start(xr[:, n * HT:(n + 1) * HT, :], src).then_inc(x_in[n], 16)
                for pc in range(4):
                    sp.wait_ge(qkv_lo, b * 24 + 4 * pc + 4)
                    dst, parts = (stq, (0, 0, 1)) if pc < 2 else (stk, (0, 1, 0))
                    for g in range(HPC):
                        for r, part in enumerate(parts):
                            h0 = (pc % 2) * 2 * HPC + g
                            sp.dma_start(dst[r * DH:(r + 1) * DH, h0:h0 + HPC + 1:HPC, :],
                                         stg[g * DH:(g + 1) * DH, pc % 2, part, :, :]).then_inc(stacked[pc % 2], 16)
                sp.wait_ge(m_lo, b + 1)
                for l in range(2):
                    sp.dma_start(stq[3 * DH + l:3 * DH + l + 1, :, :].rearrange("o h (i q) -> o (h i) q", q=P),
                                 mrow[:, l, :]).then_inc(m_rows, 16)
                for t in range(NT + 3):
                    if t < NT:
                        row = b * SEQ + t * P
                        sp.wait_ge(x1_ready, b * NT + t + 1)
                        sp.dma_start(x1_d[bass.ds(row, P), :], xr[:, t, :]).then_inc(x1_out, 16)
                        sp.wait_ge(xn2_ready, b * NT + t + 1)
                        sp.dma_start(xw_d[bass.ds(row, P), 0:D], xn[:, t % 2, :]).then_inc(xn_out[t % 2], 16)
                    if t >= 3:
                        row = b * SEQ + (t - 3) * P
                        sp.wait_ge(y_sb, b * NT + t - 3 + 1)
                        sp.dma_start(y_d[bass.ds(row, P), :], ysh[:, (t - 3) % 2, :]).then_inc(y_out[(t - 3) % 2], 16)
                sp.wait_ge(wgt_ready, b + 1)
                sp.dma_start(xw_d[bass.ds(b * SEQ, SEQ), D:XW].rearrange("(t p) e -> p t e", p=P), wgt).then_inc(wgt_out, 16)
                sp.wait_ge(x1_out, b * (16 * NT) + 16 * NT + 16)
                hold("sp", sp, wgt_out, b * 16 + 16)
            experts_sync(sp)


        @block.gpsimd
        def _(pool):
            g = nc.gpsimd
            inc = lambda i: i.then_inc(s_const, 1)
            inc(g.memset(ident[:, :], 0.0))
            inc(g.memset(ident_b[:, :], 0.0))
            inc(g.memset(mask_qk[:, :], 0.0))
            inc(g.memset(mask_kq[:, :], 0.0))
            inc(g.memset(earlier[:, :], 1.0))
            inc(g.memset(ones_b[:, :], 1.0))
            inc(g.memset(mhalf[:, :], -0.5))
            inc(g.memset(zeros_row[:, :], 0.0))
            pool.wait_ge(s_const, 8)
            aff = lambda t, cmp, fill, base, cm, st: inc(g.affine_select(
                out=t[:, :], in_=t[:, :], compare_op=cmp, fill=fill, base=base, pattern=[[st, P]], channel_multiplier=cm))
            aff(ident, ALU.not_equal, 1.0, 0, 1, -1)
            aff(ident_b, ALU.not_equal, 1.0, 0, 1, -1)
            aff(mask_qk, ALU.is_ge, -BIG, 0, 1, -1)
            aff(mask_kq, ALU.is_ge, -BIG, 0, -1, 1)
            aff(earlier, ALU.is_ge, 0.0, -1, -1, 1)
            inc(g.iota(slot_init[:, :], pattern=[[0, E]], base=TOK, channel_multiplier=1))
            inc(g.iota(tok_i[:, :], pattern=[[P, NT]], base=0, channel_multiplier=1))
            inc(g.iota(cols_i[:, :], pattern=[[1, E]], base=0, channel_multiplier=0))

            def put_slots(b):
                hold("pool", pool, slot_ready, b + 1)
                for t in range(NT):
                    for k in range(K):
                        g.indirect_dma_start(
                            out=slot_d, out_offset=bass.IndirectOffsetOnAxis(ap=slot_i[:, t, k:k + 1], axis=0),
                            in_=tok_i[:, t:t + 1], in_offset=None, bounds_check=CAP * E - 1,
                            oob_is_err=False).then_inc(slot_put, 16)

            def first_norm(b):
                hold("pool", pool, ln_stat, b + 1)
                g.tensor_scalar(ve[:, :], mv[:, :, 1], EPS, None, ALU.add).then_inc(ln_eps, 1)
                hold("pool", pool, ln_eps, b + 1)
                g.tensor_tensor(rstd[:, :], ve[:, :], mhalf[:, :], ALU.pow).then_inc(ln_rstd, 1)

            def later_norms(b):
                for t in range(NT):
                    for k in range(2):
                        n = 2 * t + k
                        eps = EPS * (S_V * S_W) ** 2 if k == 0 else EPS
                        c = n % 4
                        hold("pool", pool, statv, b * (2 * NT) + n + 1)
                        g.tensor_scalar(ve2[:, c:c + 1], mv2[:, c, 1:2], eps, None, ALU.add).then_inc(pow_in, 1)
                        hold("pool", pool, pow_in, b * (2 * NT) + n + 1)
                        g.tensor_tensor(rs2[:, c:c + 1], ve2[:, c:c + 1], mhalf[:, 0:1], ALU.pow).then_inc(pow_out, 1)

            def count_before(b):
                hold("pool", pool, sel_ready, b + 1)
                for t in range(NT):
                    g.tensor_copy(before_b[:, t, :], carry[:, :]).then_inc(r_carry, 1)
                    hold("pool", pool, r_carry, b * (2 * NT) + 2 * t + 1)
                    g.tensor_tensor(carry[:, :], carry[:, :], sel[:, t, :], ALU.add).then_inc(r_carry, 1)
                    hold("pool", pool, r_carry, b * (2 * NT) + 2 * t + 2)

            pool.wait_ge(s_const, N_CONST)
            pool.wait_ge(s_vconst, 5)
            pool.wait_ge(s_init, 32)
            pool.sem_inc(tok_ready, 1)
            pool.sem_inc(oe_free, 2)
            first_norm(0)
            with pool.Fori(0, NB - 1) as b:
                later_norms(b)
                count_before(b)
                first_norm(b + 1)
                put_slots(b)
                hold("pool", pool, slot_put, b * (16 * NT * K) + 16 * NT * K)
                g.tensor_scalar(tok_f[:, :], tok_i[:, :], float(SEQ), None, ALU.add).then_inc(tok_ready, 1)
                hold("pool", pool, tok_ready, 2 * b + 2)
                g.tensor_copy(tok_i[:, :], tok_f[:, :]).then_inc(tok_ready, 1)
                hold("pool", pool, tok_ready, 2 * b + 3)
            later_norms(NB - 1)
            count_before(NB - 1)
            put_slots(NB - 1)
            experts_pool(pool)

        @block.scalar
        def _(act):
            a = nc.scalar
            act.wait_ge(s_wld, 16 * 8)
            for src, dst, parts in SPLITS:
                a.activation(dst[:, 0], src, ACT.Copy, scale=S_W).then_inc(s_whi, 1)

            def exps(b, h, peeled):
                for gi in range(NG):
                    n = NG * (b * NH + h) + gi
                    _, w = group_blocks(gi)
                    act.wait_ge(st_psum, n + 1)
                    if not (peeled and gi < 2):
                        act.wait_ge(pl_done, n - 1)
                    a.activation(p32[:, gi % 2, 0:w], bank(2 * (gi % 2), w), ACT.Exp, bias=ln_sp[:, 0:1],
                                 scale=SM_SCALE).then_inc(exp_done, 1)
                    if not ph_by_dve[gi]:
                        if not (peeled and gi < 3):
                            act.wait_ge(pv_done, n - 2)
                        act.wait_ge(exp_done, n + 1)
                        a.activation(phl[:, gi % 3, 0, 0:w], p32[:, gi % 2, 0:w], ACT.Copy).then_inc(ph_act, 1)
                    if gi == 2 and not peeled:
                        act.wait_ge(pv_done, NG * (b * NH + h))
                        a.activation(olo[:, 1, :, :], o_bank(1)[:, :, DH + 1:2 * DH + 1], ACT.Copy).then_inc(olo_done, 1)
                    if gi == 4:
                        act.wait_ge(pv_done, NG * (b * NH + h) + 2)
                        a.activation(olo[:, 0, :, :], o_bank(0)[:, :, DH + 1:2 * DH + 1], ACT.Copy).then_inc(olo_done, 1)

            with act.Fori(0, NB) as b:
                for t in range(NT):
                    act.wait_ge(xt_psum, b * NT + t + 1)
                    a.activation(xT[:, 0, :, t * P:(t + 1) * P], bank(6 + t % 2).rearrange("p (c s) -> p c s", c=C),
                                 ACT.Copy, scale=S_X).then_inc(xt_hi, 1)
                for n in range(24):
                    act.wait_ge(qkv_psum, b * 24 + n + 1)
                    if n < 16:
                        if n % 4 == 0 and n >= 8:
                            act.wait_ge(stacked[(n // 4) % 2], b * (2 * 16 * 12) + 16 * 12)
                        a.activation(stg[:, (n // 4) % 2, 0, (n // 2) % 2, (n % 2) * 512:(n % 2) * 512 + 512], bank(n % 4),
                                     ACT.Copy, scale=S_QK / (S_X * S_W)).then_inc(qkv_hi, 1)
                    else:
                        a.activation(vv[:, n - 16, :, 0:DH], bank(n % 4).rearrange("p (h d) -> p h d", h=NH),
                                     ACT.Copy, scale=S_V / (S_X * S_W)).then_inc(qkv_hi, 1)
                act.wait_ge(mt_psum, b + 1)
                a.activation(mrow[:, 0, :], bank(6, P), ACT.Copy, scale=-1.0 / M_HI).then_inc(m_hi, 1)
                exps(b, 0, True)
                with act.Fori(1, NH) as h:
                    exps(b, h, False)
                act.wait_ge(pv_done, NG * (b * NH + NH))
                a.activation(olo[:, 1, :, :], o_bank(1)[:, :, DH + 1:2 * DH + 1], ACT.Copy).then_inc(olo_done, 1)
                for s in range(NT + 3):
                    if s < NT:
                        act.wait_ge(to_psum, b * NT + s + 1)
                        if s >= 2:
                            act.wait_ge(a_psum, b * NT + s - 1)
                        a.activation(oT[:, s % 2, 0, :], bank(6), ACT.Copy).then_inc(ot_hi, 1)
                    if 2 <= s < NT + 2:
                        act.wait_ge(ff_psum, b * NT + s - 2 + 1)
                        if s > 2:
                            act.wait_ge(h_ready, b * NT + s - 2)
                        a.activation(gex[:, :], bank(2 + s % 2, FF + E), ACT.Exp, scale=-1.0 / (S_X * S_W)).then_inc(ff_exp, 1)
                    if s >= 3:
                        t = s - 3
                        act.wait_ge(dn_psum, b * NT + t + 1)
                        if t >= 2:
                            act.wait_ge(y_out[t % 2], (b * (NT // 2) + t // 2) * 16)
                        a.activation(ysh[:, t % 2, :], bank(4), ACT.Copy, scale=1.0 / (S_H * S_W)).then_inc(y_sb, 1)
                    if 2 <= s < NT + 2:
                        act.wait_ge(th_psum, b * NT + s - 2 + 1)
                        if s >= 3:
                            act.wait_ge(dn_psum, b * NT + s - 2)
                        sc_h = S_H / (S_X * S_W) ** 2
                        a.activation(hT[:, 0, 0, :], bank(5, P), ACT.Copy, scale=sc_h).then_inc(ht_hi, 1)
                        a.activation(hT[0:FR, 0, 1, :], bank(5, P, P)[0:FR], ACT.Copy, scale=sc_h).then_inc(ht_hi, 1)
                    if 1 <= s < NT + 1:
                        act.wait_ge(tx_psum, b * NT + s - 1 + 1)
                        if s >= 3:
                            act.wait_ge(ff_psum, b * NT + s - 2)
                        a.activation(x2T[:, (s - 1) % 2, 0, :], bank(7), ACT.Copy, scale=S_X).then_inc(x2_hi, 1)
                for n in range(2):
                    act.wait_ge(y_out[n], (b * (NT // 2) + NT // 2) * 16)
            experts_act(act)

        def routing(dve, b):
            v = nc.vector
            k = [0]

            def link(ins):
                k[0] = k[0] + 1
                ins.then_inc(r_step, 1)
                hold("dve", dve, r_step, b * RS + k[0])

            def step(ins):
                k[0] = k[0] + 1
                ins.then_inc(r_step, 1)

            n8 = NT * G
            link(v.tensor_tensor(scb, sc, bias_b[:, :].rearrange("p (o e) -> p o e", o=1).to_broadcast((P, NT, E)), ALU.add))
            gx = scb.rearrange("p t (g m) -> p (t g) m", g=G)
            hi1 = cand.rearrange("p t (g m) -> p (t g) m", g=G)[:, :, 0:4]
            lo1 = cand.rearrange("p t (g m) -> p (t g) m", g=G)[:, :, 4:8]
            step(v.tensor_tensor(hi1, gx[:, :, 0:4], gx[:, :, 4:8], ALU.max))
            link(v.tensor_tensor(lo1, gx[:, :, 0:4], gx[:, :, 4:8], ALU.min))
            rg = rest.rearrange("p t (g m) -> p (t g) m", g=G)
            step(v.tensor_tensor(rg[:, :, 0:2], hi1[:, :, 0:2], hi1[:, :, 2:4], ALU.max))
            step(v.tensor_tensor(rg[:, :, 2:4], hi1[:, :, 0:2], hi1[:, :, 2:4], ALU.min))
            link(v.tensor_tensor(rg[:, :, 4:6], lo1[:, :, 0:2], lo1[:, :, 2:4], ALU.max))
            link(v.tensor_tensor(rg[:, :, 6:8], rg[:, :, 2:4], rg[:, :, 4:6], ALU.max))
            wg = wgt.rearrange("p t (g m) -> p (t g) m", g=G)
            step(v.tensor_tensor(wg[:, :, 0:1], rg[:, :, 0:1], rg[:, :, 1:2], ALU.max))
            step(v.tensor_tensor(wg[:, :, 1:2], rg[:, :, 0:1], rg[:, :, 1:2], ALU.min))
            link(v.tensor_tensor(wg[:, :, 2:3], rg[:, :, 6:7], rg[:, :, 7:8], ALU.max))
            link(v.tensor_tensor(wg[:, :, 3:4], wg[:, :, 1:2], wg[:, :, 2:3], ALU.max))
            wt = wgt.rearrange("p t (g m) -> p t g m", g=G)
            link(v.tensor_tensor(gpad[:, :, 0:G], wt[:, :, :, 0], wt[:, :, :, 3], ALU.add))
            for t in range(NT):
                step(v.max(top8[:, t, :], gpad[:, t, :]))
            hold("dve", dve, r_step, b * RS + k[0])
            link(v.memset(top8[:, :, KG:8], -BIG))
            for t in range(NT):
                step(v.match_replace(gout[:, t, :], top8[:, t, :], gpad[:, t, :], -BIG))
            hold("dve", dve, r_step, b * RS + k[0])
            gm = gmask[:, :].rearrange("p (t g) -> p t g", t=NT)
            link(v.tensor_tensor(gm, gout[:, :, 0:G], gpad[:, :, 0:G], ALU.not_equal))
            link(v.tensor_scalar(gneg[:, :], gmask[:, :], BIG, BIG, ALU.mult, ALU.subtract))
            cg = cand.rearrange("p t (g m) -> p (t g) m", g=G)
            link(v.tensor_tensor(cg, gx, gmask[:, :].rearrange("p (n o) -> p n o", o=1).to_broadcast((P, n8, 8)), ALU.mult))
            link(v.tensor_tensor(cg, cg, gneg[:, :].rearrange("p (n o) -> p n o", o=1).to_broadcast((P, n8, 8)), ALU.add))
            for t in range(NT):
                step(v.max(top8[:, t, :], cand[:, t, :]))
            hold("dve", dve, r_step, b * RS + k[0])
            link(v.memset(top8[:, :, K:8], -BIG))
            for t in range(NT):
                step(v.match_replace(rest[:, t, :], top8[:, t, :], cand[:, t, :], -BIG))
            hold("dve", dve, r_step, b * RS + k[0])
            link(v.tensor_tensor(sel, rest, cand, ALU.not_equal))
            step(v.tensor_copy(sel_b, sel))
            v.tensor_tensor(wgt, sc, sel, ALU.mult).then_inc(sel_ready, 1)
            dve.wait_ge(sel_ready, b + 1)
            link(v.reduce_sum(wsum[:, :, :], wgt, AX_X))
            link(v.reciprocal(wsum[:, :, :], wsum[:, :, :]))
            v.scalar_tensor_tensor(out=wgt, in0=wgt, scalar=ROUTE_SCALE, in1=wsum[:, :, :].to_broadcast((P, NT, E)),
                                   op0=ALU.mult, op1=ALU.mult).then_inc(wgt_ready, 1)
            dve.wait_ge(pos_psum, b + 1)
            pos = bank(6, NT * E).rearrange("p (t e) -> p t e", t=NT)
            step(v.scalar_tensor_tensor(out=rest, in0=pos, scalar=float(CAP), in1=sel, op0=ALU.is_lt, op1=ALU.mult))
            link(v.scalar_tensor_tensor(out=neg, in0=pos, scalar=-float(E),
                                        in1=slot_e[:, :].rearrange("p (o e) -> p o e", o=1).to_broadcast((P, NT, E)),
                                        op0=ALU.mult, op1=ALU.subtract))
            link(v.scalar_tensor_tensor(out=neg, in0=neg, scalar=NO_SLOT, in1=rest, op0=ALU.add, op1=ALU.mult))
            link(v.tensor_scalar(neg, neg, -NO_SLOT, None, ALU.add))
            for t in range(NT):
                step(v.max(top8[:, t, :], neg[:, t, :]))
            hold("dve", dve, r_step, b * RS + k[0])
            dve.wait_ge(tok_ready, 2 * b + 1)
            v.tensor_scalar(slot_i[:, :, :], top8[:, :, :], -1.0, None, ALU.mult).then_inc(slot_ready, 1)
            assert k[0] == RS, k[0]

        @block.vector
        def _(dve):
            v = nc.vector
            vi = lambda i: i.then_inc(s_vconst, 1)
            vi(v.memset(ln_sp[:, :], LN_SP))
            vi(v.memset(vv[:, :, :, DH:DH + 1], 1.0))
            vi(v.memset(gpad[:, :, :], -BIG))
            vi(v.memset(carry[:, :], 0.0))
            dve.wait_ge(s_const, N_CONST)
            vi(v.tensor_copy(slot_e[:, :], cols_i[:, :]))
            for n, (src, dst, parts) in enumerate(SPLITS):
                dve.wait_ge(s_whi, n + 1)
                v.scalar_tensor_tensor(out=dst[:, 1], in0=src, scalar=S_W, in1=dst[:, 0], op0=ALU.mult,
                                       op1=ALU.subtract).then_inc(s_wlo, 1)
            dve.wait_ge(s_wlo, len(SPLITS))
            vi(v.memset(stq[3 * DH:P, :, :], 0.0))
            vi(v.memset(stk[3 * DH:P, :, :], 0.0))
            dve.wait_ge(s_vconst, 7)
            vi(v.memset(stk[3 * DH:3 * DH + 2, :, :], -1.0))
            dve.wait_ge(s_vconst, 8)
            vi(v.memset(stk[3 * DH:3 * DH + 1, :, :], M_HI))
            dve.wait_ge(s_vconst, 9)

            def probs(b, h, peeled):
                for gi in range(NG):
                    n = NG * (b * NH + h) + gi
                    _, w = group_blocks(gi)
                    dve.wait_ge(exp_done, n + 1)
                    if not (peeled and gi < 3):
                        dve.wait_ge(pv_done, n - 2)
                    if ph_by_dve[gi]:
                        k = n_ph_dve * (b * NH + h) + sum(ph_by_dve[:gi + 1])
                        v.tensor_copy(phl[:, gi % 3, 0, 0:w], p32[:, gi % 2, 0:w]).then_inc(ph_dve, 1)
                        dve.wait_ge(ph_dve, k)
                    else:
                        dve.wait_ge(ph_act, n_ph_act * (b * NH + h) + gi + 1 - sum(ph_by_dve[:gi + 1]))
                    v.tensor_tensor(phl[:, gi % 3, 1, 0:w], p32[:, gi % 2, 0:w], phl[:, gi % 3, 0, 0:w],
                                    ALU.subtract).then_inc(pl_done, 1)
                    if gi == 2 and not peeled:
                        attn_out(2 * (b * NH + h) - 1, h - 1, 1)
                    if gi == 4:
                        attn_out(2 * (b * NH + h), h, 0)

            def attn_out(n, h, half):
                dve.wait_ge(olo_done, n + 1)
                ob = o_bank(half)
                v.tensor_tensor(osum[:, :, :], ob[:, :, 0:DH], olo[:, half, :, :], ALU.add).then_inc(o_step, 1)
                v.reciprocal(orec[:, :, :], ob[:, :, DH:DH + 1]).then_inc(o_step, 1)
                dve.wait_ge(o_step, 2 * n + 2)
                v.tensor_tensor(o_sb[:, half * HT:(half + 1) * HT, bass.ds(h * DH, DH)], osum[:, :, :],
                                orec[:, :, :].to_broadcast((P, HT, DH)), ALU.mult).then_inc(o_done, 1)

            with dve.Fori(0, NB) as b:
                for t in range(NT):
                    if t % HT == 0:
                        dve.wait_ge(x_in[t // HT], b * 16 + 16)
                    v.bn_stats(stats[:, t, :], xr[:, t, :]).then_inc(x1_step, 1)
                hold("dve", dve, x1_step, b * X1S + NT)
                for t in range(NT):
                    ins = v.bn_aggr(mv[:, t, :], stats[:, t, :])
                ins.then_inc(ln_stat, 1)
                dve.wait_ge(ln_rstd, b + 1)
                for s in range(NT + 1):
                    if s < NT:
                        if s >= 2:
                            dve.wait_ge(xt_psum, b * NT + s - 1)
                        v.tensor_scalar(xn[:, s % 2, :], xr[:, s, :], mv[:, s, 0:1], rstd[:, s:s + 1],
                                        ALU.subtract, ALU.mult).then_inc(xn_ready, 1)
                    if s >= 1:
                        t = s - 1
                        dve.wait_ge(xt_hi, b * NT + t + 1)
                        v.scalar_tensor_tensor(out=xT[:, 1, :, t * P:(t + 1) * P],
                                               in0=bank(6 + t % 2).rearrange("p (c s) -> p c s", c=C), scalar=S_X,
                                               in1=xT[:, 0, :, t * P:(t + 1) * P], op0=ALU.mult,
                                               op1=ALU.subtract).then_inc(xt_lo, 1)
                for n in range(24):
                    dve.wait_ge(qkv_hi, b * 24 + n + 1)
                    if n < 16:
                        sl = lambda l: stg[:, (n // 4) % 2, l, (n // 2) % 2, (n % 2) * 512:(n % 2) * 512 + 512]
                        v.scalar_tensor_tensor(out=sl(1), in0=bank(n % 4), scalar=S_QK / (S_X * S_W), in1=sl(0),
                                               op0=ALU.mult, op1=ALU.subtract).then_inc(qkv_lo, 1)
                    else:
                        v.scalar_tensor_tensor(out=vv[:, n - 16, :, DH + 1:2 * DH + 1],
                                               in0=bank(n % 4).rearrange("p (h d) -> p h d", h=NH),
                                               scalar=S_V / (S_X * S_W), in1=vv[:, n - 16, :, 0:DH],
                                               op0=ALU.mult, op1=ALU.subtract).then_inc(qkv_lo, 1)
                with dve.Fori(0, NH) as h:
                    for i in range(NT):
                        dve.wait_ge(s_psum, NT * (b * NH + h) + i + 1)
                        v.tensor_reduce(mx[:, bass.ds(h * NT + i, 1)], PS[:, (i % 4) * 1024:(i % 4) * 1024 + (i + 1) * P],
                                        AX_X, ALU.max).then_inc(max_done, 1)
                dve.wait_ge(m_hi, b + 1)
                v.scalar_tensor_tensor(out=mrow[:, 1, :], in0=mrow[:, 0, :], scalar=M_HI, in1=bank(6, P),
                                       op0=ALU.mult, op1=ALU.add).then_inc(m_lo, 1)
                probs(b, 0, True)
                with dve.Fori(1, NH) as h:
                    probs(b, h, False)
                attn_out(2 * (b * NH + NH) - 1, NH - 1, 1)

                k1, k2 = [NT], [0]

                def link(ins):
                    k1[0] += 1
                    ins.then_inc(x1_step, 1)
                    hold("dve", dve, x1_step, b * X1S + k1[0])

                def hlink(ins):
                    k2[0] += 1
                    ins.then_inc(h_step, 1)
                    dve.wait_ge(h_step, b * HS + k2[0])

                for s in range(NT + 3):
                    if s < NT:
                        dve.wait_ge(ot_hi, b * NT + s + 1)
                        v.tensor_tensor(oT[:, s % 2, 1, :], bank(6), oT[:, s % 2, 0, :], ALU.subtract).then_inc(ot_lo, 1)
                    if 2 <= s < NT + 2:
                        t = s - 2
                        dve.wait_ge(ff_exp, b * NT + t + 1)
                        fb = bank(2 + t % 2, FW)
                        hlink(v.tensor_scalar(gex[:, :], gex[:, :], 1.0, None, ALU.add))
                        v.reciprocal(sc[:, t, :], gex[:, FF:FF + E]).then_inc(h_step, 1)
                        k2[0] += 1
                        hlink(v.reciprocal(grc[:, :], gex[:, 0:FF]))
                        if t >= 1:
                            dve.wait_ge(th_psum, b * NT + t)
                        hlink(v.tensor_tensor(hid[:, :], fb[:, 0:FF], grc[:, :], ALU.mult))
                        v.tensor_tensor(hid[:, :], fb[:, FF + E:FW], hid[:, :], ALU.mult).then_inc(h_ready, 1)
                    if s < NT:
                        dve.wait_ge(a_psum, b * NT + s + 1)
                        c = (2 * s) % 4
                        link(v.bn_stats(st2[:, c, :], bank(s % 2)))
                        v.bn_aggr(mv2[:, c, :], st2[:, c, :]).then_inc(statv, 1)
                    if 2 <= s < NT + 2:
                        t = s - 2
                        sc_h = S_H / (S_X * S_W) ** 2
                        dve.wait_ge(ht_hi, 2 * (b * NT + t) + 2)
                        v.scalar_tensor_tensor(out=hT[:, 1, 0, :], in0=bank(5, P), scalar=sc_h, in1=hT[:, 0, 0, :],
                                               op0=ALU.mult, op1=ALU.subtract).then_inc(ht_lo, 1)
                        v.scalar_tensor_tensor(out=hT[0:FR, 1, 1, :], in0=bank(5, P, P)[0:FR], scalar=sc_h,
                                               in1=hT[0:FR, 0, 1, :], op0=ALU.mult, op1=ALU.subtract).then_inc(ht_lo, 1)
                    if s < NT:
                        dve.wait_ge(pow_out, b * (2 * NT) + 2 * s + 1)
                        c = (2 * s) % 4
                        if s >= 2:
                            dve.wait_ge(xn_out[s % 2], (b * (NT // 2) + s // 2) * 16)
                            dve.wait_ge(tx_psum, b * NT + s - 1)
                        link(v.tensor_scalar(xn[:, s % 2, :], bank(s % 2), mv2[:, c, 0:1], rs2[:, c:c + 1],
                                             ALU.subtract, ALU.mult))
                        v.tensor_tensor(xr[:, s, :], xr[:, s, :], xn[:, s % 2, :], ALU.add).then_inc(x1_ready, 1)
                        dve.wait_ge(x1_ready, b * NT + s + 1)
                        link(v.bn_stats(st2[:, c + 1, :], xr[:, s, :]))
                        v.bn_aggr(mv2[:, c + 1, :], st2[:, c + 1, :]).then_inc(statv, 1)
                    if 1 <= s < NT + 1:
                        t = s - 1
                        dve.wait_ge(x2_hi, b * NT + t + 1)
                        v.scalar_tensor_tensor(out=x2T[:, t % 2, 1, :], in0=bank(7), scalar=S_X, in1=x2T[:, t % 2, 0, :],
                                               op0=ALU.mult, op1=ALU.subtract).then_inc(x2_lo, 1)
                    if s < NT:
                        dve.wait_ge(pow_out, b * (2 * NT) + 2 * s + 2)
                        v.tensor_scalar(xn[:, s % 2, :], xr[:, s, :], mv2[:, c + 1, 0:1], rs2[:, c + 1:c + 2],
                                        ALU.subtract, ALU.mult).then_inc(xn2_ready, 1)
                for n in range(2):
                    dve.wait_ge(xn_out[n], (b * (NT // 2) + NT // 2) * 16)
                routing(dve, b)
            experts_dve(dve)

        @block.tensor
        def _(pe):
            def mm(o, l, r, start, stop, **kw):
                return nc.tensor.matmul(o, l, r, start=start, stop=stop, **kw)

            def split3(o, lhs, rhs, n=C):
                k = 0
                for c in range(n):
                    for l, r in ((0, 0), (0, 1), (1, 0)):
                        ins = mm(o, lhs(l, c), rhs(r, c), k == 0, k == 3 * n - 1)
                        k += 1
                return ins

            pe.wait_ge(s_const, N_CONST)
            pe.wait_ge(s_wlo, len(SPLITS))
            pe.wait_ge(s_vconst, 9)

            def scores_max(b, h, peeled):
                for i in range(NT):
                    n = NT * (b * NH + h) + i
                    if not (peeled and i < 4):
                        pe.wait_ge(max_done, n - 3)
                    base = (i % 4) * 1024
                    w = (i + 1) * P
                    for c0 in range(0, w, 512):
                        cw = min(512, w - c0)
                        ins = mm(PS[:, base + c0:base + c0 + cw], stq[0:3 * DH, h, i * P:(i + 1) * P],
                                 stk[0:3 * DH, h, c0:c0 + cw], True, True, skip_group_check=True)
                    ins = mm(PS[:, base + w - P:base + w], ident_b[:, :], mask_qk[:, :], False, True,
                             skip_group_check=True)
                    ins.then_inc(s_psum, 1)

            def scores_t(b, h, gi, peeled):
                n = NG * (b * NH + h) + gi
                if not (peeled and gi < 2):
                    pe.wait_ge(exp_done, n - 1)
                blocks, _ = group_blocks(gi)
                base = 2 * (gi % 2) * 512
                for q, (j, i0, w, col) in enumerate(blocks):
                    diag = j == i0
                    ins = mm(PS[:, base + col:base + col + w], stk[:, h, j * P:(j + 1) * P],
                             stq[:, h, i0 * P:i0 * P + w], col % 512 == 0, True, skip_group_check=True)
                    if diag:
                        ins = mm(PS[:, base + col:base + col + P], ident_b[:, :], mask_kq[:, :], False, True,
                                 skip_group_check=True)
                ins.then_inc(st_psum, 1)

            def values(b, h, gi, n, peeled):
                half = GROUPS[gi][0]
                blocks, _ = group_blocks(gi)
                pe.wait_ge(pl_done, n + 1)
                first = gi == 0 or GROUPS[gi - 1][0] != half
                if first and not peeled:
                    pe.wait_ge(o_done, 2 * (b * NH + h) - 1 + half)
                ob = o_bank(half)
                for j, i0, w, col in blocks:
                    for q in range(w // P):
                        i = i0 + q - half * HT
                        for l in range(2):
                            wcols = 2 * DH + 1
                            ins = mm(ob[:, i, 0:wcols], phl[:, gi % 3, l, col + q * P:col + (q + 1) * P],
                                     vv[:, j, h, 0:wcols], first and j == blocks[0][0] and q == 0 and l == 0, True,
                                     skip_group_check=True)
                ins.then_inc(pv_done, 1)

            def transposes(o, src, w=P):
                for c in range(C):
                    ins = nc.tensor.transpose(o[:, c * P:(c + 1) * P], src[:, c * P:(c + 1) * P], ident[:, :])
                return ins

            with pe.Fori(0, NB) as b:
                for t in range(NT):
                    pe.wait_ge(xn_ready, b * NT + t + 1)
                    if t >= 2:
                        pe.wait_ge(xt_lo, b * NT + t - 1)
                    transposes(bank(6 + t % 2), xn[:, t % 2, :]).then_inc(xt_psum, 1)
                for n in range(24):
                    if n == 0:
                        pe.wait_ge(xt_lo, b * NT + HT)
                    if n == 1:
                        pe.wait_ge(xt_lo, b * NT + NT)
                    if n >= 4:
                        pe.wait_ge(qkv_lo, b * 24 + n - 3)
                    if n < 16:
                        oc, s0 = n // 2, (n % 2) * 512
                        ins = split3(bank(n % 4), lambda l, c: wqkv[:, l, c, oc * P:(oc + 1) * P],
                                     lambda l, c: xT[:, l, c, s0:s0 + 512])
                    else:
                        t = n - 16
                        ins = split3(bank(n % 4), lambda l, c: xT[:, l, c, t * P:(t + 1) * P],
                                     lambda l, c: wqkv[:, l, c, 2 * D:3 * D])
                    ins.then_inc(qkv_psum, 1)
                for n in range(2):
                    pe.wait_ge(stacked[n], b * (2 * 16 * 12) + 2 * 16 * 12)
                pe.wait_ge(qkv_lo, b * 24 + 24)
                scores_max(b, 0, True)
                with pe.Fori(1, NH) as h:
                    scores_max(b, h, False)
                pe.wait_ge(max_done, NT * (b * NH + NH))
                nc.tensor.transpose(bank(6, P), mx[:, :], ident[:, :]).then_inc(mt_psum, 1)
                pe.wait_ge(m_rows, b * 32 + 32)
                for gi in range(NG):
                    scores_t(b, 0, gi, True)
                    if gi >= 2:
                        values(b, 0, gi - 2, NG * (b * NH) + gi - 2, True)
                with pe.Fori(1, NH) as h:
                    for gi in range(NG):
                        scores_t(b, h, gi, False)
                        g0 = (gi - 2) % NG
                        h0 = h if gi >= 2 else h - 1
                        values(b, h0, g0, NG * (b * NH + h) + gi - 2, gi < 2)
                for gi in (NG - 2, NG - 1):
                    values(b, NH - 1, gi, NG * (b * NH + NH - 1) + gi, True)
                pe.wait_ge(o_done, 2 * (b * NH + NH))
                for s in range(NT + 3):
                    if s < NT:
                        if s >= 1:
                            pe.wait_ge(ot_lo, b * NT + s)
                        transposes(bank(6), o_sb[:, s, :]).then_inc(to_psum, 1)
                    if 2 <= s < NT + 2:
                        t = s - 2
                        pe.wait_ge(x2_lo, b * NT + t + 1)
                        if t >= 2:
                            pe.wait_ge(h_ready, b * NT + t - 1)
                        split3(bank(2 + t % 2, FW), lambda l, c: x2T[:, t % 2, l, c * P:(c + 1) * P],
                               lambda l, c: wff[:, l, c, :]).then_inc(ff_psum, 1)
                    if s < NT:
                        pe.wait_ge(ot_lo, b * NT + s + 1)
                        if s >= 2:
                            pe.wait_ge(x1_ready, b * NT + s - 1)
                        split3(bank(s % 2), lambda l, c: oT[:, s % 2, l, c * P:(c + 1) * P],
                               lambda l, c: wo[:, l, c, :]).then_inc(a_psum, 1)
                    if s >= 3:
                        t = s - 3
                        pe.wait_ge(ht_lo, 2 * (b * NT + t) + 2)
                        if t >= 1:
                            pe.wait_ge(y_sb, b * NT + t)
                        k = 0
                        for c, kp in ((0, P), (1, FR)):
                            for l, r in ((0, 0), (0, 1), (1, 0)):
                                ins = mm(bank(4), hT[0:kp, l, c, :], wdn[0:kp, r, c, :], k == 0, k == 5)
                                k += 1
                        ins.then_inc(dn_psum, 1)
                    if 2 <= s < NT + 2:
                        t = s - 2
                        pe.wait_ge(h_ready, b * NT + t + 1)
                        if t >= 1:
                            pe.wait_ge(ht_lo, 2 * (b * NT + t))
                        nc.tensor.transpose(bank(5, P), hid[:, 0:P], ident[:, :])
                        nc.tensor.transpose(bank(5, P, P)[0:FR], hid[:, P:FF], ident[:, :]).then_inc(th_psum, 1)
                    if 1 <= s < NT + 1:
                        t = s - 1
                        pe.wait_ge(xn2_ready, b * NT + t + 1)
                        if t >= 1:
                            pe.wait_ge(x2_lo, b * NT + t)
                        transposes(bank(7), xn[:, t % 2, :]).then_inc(tx_psum, 1)
                pe.wait_ge(r_carry, b * (2 * NT) + 2 * NT)
                mm(bank(6, NT * E), earlier[:, :], sel_b.rearrange("p t e -> p (t e)"), True, False)
                mm(bank(6, NT * E), ones_b[:, :], before_b.rearrange("p t e -> p (t e)"), False, True).then_inc(pos_psum, 1)
            experts_pe(pe)


def kernel(**inputs):
    import numpy as _np
    import concourse.bacc as _bacc
    from concourse import mybir as _mybir
    from concourse.bass_utils import run_bass_kernel_spmd as _run

    nc = _bacc.Bacc("TRN2", target_bir_lowering=False, num_devices=1)
    pick = lambda name: _np.asarray(inputs[name])
    laid = {
        "x": pick("L0_attn_x"),
        "w_qkv_t": pick("L0_attn_w_project").T,
        "w_out_t": pick("L0_attn_w_out").T,
    }
    for name in ("gate_w", "bias", "w_gate", "w_up", "w_down", "ws_gate", "ws_up", "ws_down"):
        laid[name] = pick("L0_ffn_" + name)
    arrays, args = {}, []
    for name, a in laid.items():
        a = _np.ascontiguousarray(a)
        arrays[f"in_{name}_dram"] = a
        args.append(nc.dram_tensor(f"in_{name}_dram", a.shape, _mybir.dt.from_np(a.dtype), kind="ExternalInput").ap())
    shape = laid["x"].shape
    args.append(nc.dram_tensor("out_0_dram", shape, _mybir.dt.float32, kind="ExternalOutput").ap())
    sandwich_kernel(nc, *args)
    r = _run(nc, [arrays], core_ids=[0])
    return r.results[0]["out_0_dram"]
```

```python
from contextlib import ExitStack

import numpy as np

import concourse.bass as bass
from concourse import mybir

P = 128
F32 = mybir.dt.float32
F16 = mybir.dt.float16
BF16 = mybir.dt.bfloat16
U32 = mybir.dt.uint32
ALU = mybir.AluOpType
ACT = mybir.ActivationFunctionType
AX_X = mybir.AxisListType.X

S_X = 16.0
S_W = 64.0
S_QK = 4.0
S_V = 16.0
S_P = 1024.0
S_H = 64.0
M_HI = 4096.0
BIG = 1.0e30
NO_SLOT = 1.0e6


def sandwich_kernel(nc, x, w_qkv_t, w_out_t, gate_w, bias, w_gate, w_up, w_down, ws_gate, ws_up, ws_down, out):
    NB, SEQ, D = x.shape
    NT = SEQ // P
    C = D // P
    NH = 16
    DH = D // NH
    E = gate_w.shape[1]
    FF = w_gate.shape[2]
    FR = FF - P
    K = 6
    G, KG = 8, 4
    ROUTE_SCALE = 2.5
    CAP = 2 * (512 * K // E)
    TOK = NB * SEQ
    XW = D + E
    HPC = P // DH
    EPS = 1e-5
    FW = 2 * FF + E
    VC = 2 * DH + 2
    HALF = SEQ // 2
    HT = HALF // P
    SM_SCALE = float(DH) ** -0.5 / (S_QK * S_QK)
    LN_SP = 6.931471805599453

    GROUPS = []
    for half in range(2):
        for j in range(0, (half + 1) * HT, 2):
            GROUPS.append((half, [(jj, max(jj, half * HT)) for jj in (j, j + 1)]))
    NG = len(GROUPS)

    def group_blocks(g):
        half, blocks = GROUPS[g]
        res, col = [], 0
        for j, i0 in blocks:
            w = ((half + 1) * HT - i0) * P
            if col // 512 != (col + w - 1) // 512:
                col = (col + 511) // 512 * 512
            res.append((j, i0, w, col))
            col += w
        return res, col

    xw_d = nc.dram_tensor("xw_rows", (TOK + P, XW), F32, kind="Internal").ap()
    x1_d = nc.dram_tensor("x_after_attention", (TOK, D), F32, kind="Internal").ap()
    y_d = nc.dram_tensor("ffn_rows", (TOK + P, D), F32, kind="Internal").ap()
    slot_d = nc.dram_tensor("token_of_slot", (CAP * E, 1), U32, kind="Internal").ap()

    outf = out.rearrange("b s d -> (b s) d")
    xf = x.rearrange("b s d -> (b s) d")

    with ExitStack() as ctx:
        def sb(name, cols, dt=F32, parts=P):
            return ctx.enter_context(nc.sbuf_tensor(name, [parts, cols], dt))

        def sem(name):
            return ctx.enter_context(nc.semaphore(name))

        def view(region, off, cols, dt=F32):
            words = cols * (4 if dt in (F32, U32) else 2) // 4
            ap = region[:, off:off + words]
            return ap if dt == F32 else ap.bitcast(dt)

        wqkv = sb("wqkv", 2 * C * 3 * D, F16)[:, :].rearrange("p (l c o) -> p l c o", l=2, c=C)
        wo = sb("wo", 2 * C * D, F16)[:, :].rearrange("p (l c o) -> p l c o", l=2, c=C)
        wff = sb("wff", 2 * C * FW, F16)[:, :].rearrange("p (l c o) -> p l c o", l=2, c=C)
        wdn = sb("wdn", 2 * 2 * D, F16)[:, :].rearrange("p (l c o) -> p l c o", l=2, c=2)
        ident = sb("ident", P)
        ident_b = sb("ident_b", P, BF16)
        mask_qk = sb("mask_qk", P, BF16)
        mask_kq = sb("mask_kq", P, BF16)
        earlier = sb("earlier", P, BF16)
        ones_b = sb("ones_b", P, BF16)
        bias_b = sb("bias_b", E)
        slot_e = sb("slot_e", E)
        mhalf = sb("mhalf", NT)
        ln_sp = sb("ln_sp", 1)
        xt_reg = sb("xt_reg", C * SEQ)
        xT = xt_reg[:, :].bitcast(F16).rearrange("p (l c s) -> p l c s", l=2, c=C)
        o_reg = sb("o_reg", NT * D)
        o_sb = o_reg[:, :].rearrange("p (t d) -> p t d", t=NT)
        stack = sb("stack", NH * SEQ)
        stq = view(stack, 0, NH * SEQ, F16).rearrange("p (h s) -> p h s", h=NH)
        stk = view(stack, NH * SEQ // 2, NH * SEQ, F16).rearrange("p (h s) -> p h s", h=NH)
        stg = sb("stg", 2 * 2 * SEQ, F16)[:, :].rearrange("p (n l s) -> p n l s", n=2, l=2)
        vv = sb("vv", NT * NH * VC, F16)[:, :].rearrange("p (t h c) -> p t h c", t=NT, h=NH)
        pt = sb("pt", 6 * 1024)
        p32 = view(pt, 0, 3072).rearrange("p (n c) -> p n c", n=3)
        phl = view(pt, 3072, 3 * 2048, F16).rearrange("p (n l c) -> p n l c", n=3, l=2)
        xl_in = sb("xl_in", D)
        xl = sb("xl", D)
        lst = sb("lst", 6)
        lmv = sb("lmv", 2)
        lnr = sb("lnr", 3)
        xn = sb("xn", 2 * D)[:, :].rearrange("p (n d) -> p n d", n=2)
        mx = sb("mx", HPC * 2 * NT)[:, :].rearrange("p (h k i) -> p h k i", h=HPC, k=2)
        mxc = sb("mxc", HPC * NT)
        mrow = sb("mrow", 2 * P, F16)[:, :].rearrange("p (l q) -> p l q", l=2)
        osb = sb("osb", 2 * HT * VC)[:, :].rearrange("p (n i c) -> p n i c", n=2, i=HT)
        osum = sb("osum", 2 * HT * DH)[:, :].rearrange("p (n i d) -> p n i d", n=2, i=HT)
        orec = sb("orec", 2 * HT)[:, :].rearrange("p (n i o) -> p n i o", n=2, o=1)
        st2 = sb("st2", 4 * 6)[:, :].rearrange("p (n s) -> p n s", n=4)
        mv2 = sb("mv2", 4 * 2)[:, :].rearrange("p (n s) -> p n s", n=4)
        nr2 = sb("nr2", 4 * 3)[:, :].rearrange("p (n s) -> p n s", n=4)
        oT = view(pt, 0, 2 * 2 * D, F16).rearrange("p (n l s) -> p n l s", n=2, l=2)
        x2T = view(pt, 1024, 2 * 2 * D, F16).rearrange("p (n l s) -> p n l s", n=2, l=2)
        gex = view(pt, 2048, FF + E)
        grc = view(pt, 2304, FF)
        hid = view(pt, 2496, FF)
        hT = view(pt, 2688, 2 * 2 * P, F16).rearrange("p (l c s) -> p l c s", l=2, c=2)
        ysh = view(pt, 2944, 2 * D).rearrange("p (n d) -> p n d", n=2)
        x1 = view(pt, 3968, 2 * D).rearrange("p (n d) -> p n d", n=2)
        zeros_row = view(pt, 0, XW)
        slot_init = view(pt, XW, E, U32)
        cols_i = view(pt, XW + E, E, U32)
        tok_c = view(pt, XW + 2 * E, NT * K, U32)
        sc_t = sb("sc_t", NT * E)[:, :].rearrange("p (t e) -> p t e", t=NT)

        def rt(hf, k, dt=F32, skip=0):
            return view(o_reg, (hf * 8 + k) * HT * E + skip, HT * E, dt).rearrange("p (t e) -> p t e", t=HT)
        scb, cand, rest, sel, wgt, neg = ([rt(hf, k) for hf in range(2)] for k in range(6))
        sel_b = [rt(hf, 6, BF16) for hf in range(2)]
        before_b = [rt(hf, 6, BF16, HT * E // 2) for hf in range(2)]
        gpad = sb("gpad", HT * 2 * G)[:, :].rearrange("p (t g) -> p t g", t=HT)
        gout = sb("gout", HT * 2 * G)[:, :].rearrange("p (t g) -> p t g", t=HT)
        top8 = sb("top8", HT * 8)[:, :].rearrange("p (t g) -> p t g", t=HT)
        gmask = sb("gmask", HT * G)
        gneg = sb("gneg", HT * G)
        wsum = sb("wsum", HT)[:, :].rearrange("p (t o) -> p t o", o=1)
        carry = sb("carry", E)
        slot_i = sb("slot_i", NT * K, U32)
        tok_f = sb("tok_f", NT * K)
        tok_i = sb("tok_i", NT * K, U32)
        slot_3 = sb("slot_3", K, U32)
        tok_3 = sb("tok_3", K, U32)

        PS = ctx.enter_context(nc.psum_tensor("PS", [P, 8 * 512], F32))

        def bank(n, cols=512, first=0):
            return PS[:, n * 512 + first:n * 512 + first + cols]

        TO, TX, AO, FU, DN, TH = 0, 1, 2, 3, 6, 7

        def aux(n, cols=512):
            return bank(4 + n, cols)

        def o_bank(half):
            return bank(6 + half, HT * (2 * DH + 1)).rearrange("p (i c) -> p i c", i=HT)

        class Tiles:

            def __init__(self, first):
                self.first, self.n = first, 0

            def take(self, k=1):
                n = self.n
                self.n += k
                return self.first + n, n % 2

        LEAD = HPC + 1
        S_TILES = [(i, c) for i in range(NT) for c in range(0, (i + 1) * P, 512)]
        N_S = len(S_TILES)
        HI_BY_DVE = (1, 2, 3)
        PRO = 2 * (NT - 1)
        N_OPEN = 2 + NT + 8 + LEAD * N_S + 2
        N_LOOP = 11 * N_S + 8 + 3 * 2 + 7 * 2
        N_SEQ = N_LOOP + N_OPEN + 4
        TURNS = NT + 3
        tiles_s = [("s", h, j) for h in range(LEAD) for j in range(N_S)]
        at_m = HPC * N_S
        tiles_s[at_m:at_m] = [("in order",)]
        tiles_s[at_m + 7:at_m + 7] = [("rows",)]
        BESIDE = []
        for turn in range(TURNS):
            if turn < 2:
                BESIDE.append(([("ln",)] * (turn == 0) + [("a", turn, 0, 0), ("a", turn, 0, 1)],
                               [("a", turn, 1, 0), ("a", turn, 1, 1)], []))
            else:
                k = 6 if turn <= NT else (len(tiles_s) + 1) // 2 if turn == NT + 1 else len(tiles_s)
                mine, tiles_s = tiles_s[:k], tiles_s[k:]
                values_of = {2: [], NT + 1: [], NT + 2: [("v", NT - 2), ("v", NT - 1)]}.get(turn, [("v", turn - 3)])
                BESIDE.append((values_of, mine[:2], mine[2:]))
        assert not tiles_s

        held = {e: sem(f"held_{e}") for e in ("sp", "pool", "dve", "pe")}

        def hold(name, eng, s, value):
            eng.wait_ge(s, value)
            eng.sem_inc(held[name], 1)

        s_const = sem("s_const")
        s_vconst = sem("s_vconst")
        s_wld = sem("s_wld")
        s_whi = sem("s_whi")
        s_wlo = sem("s_wlo")
        s_rows = sem("s_rows")
        s_init = sem("s_init")
        aux_full = sem("aux_full")
        aux_free = sem("aux_free")
        x_in = sem("x_in")
        ln_st = sem("ln_st")
        ln_stat = sem("ln_stat")
        ln_eps = sem("ln_eps")
        ln_pow = sem("ln_pow")
        ln_nrm = sem("ln_nrm")
        xl_ready = sem("xl_ready")
        xt_hi = sem("xt_hi")
        v_hi = sem("v_hi")
        a_hi = sem("a_hi")
        stacked = [sem("stacked_q"), sem("stacked_k")]
        m_comb = sem("m_comb")
        m_hi = sem("m_hi")
        m_rows = sem("m_rows")
        st_psum = sem("st_psum")
        exp_done = sem("exp_done")
        ph_done = sem("ph_done")
        ph_dve = sem("ph_dve")
        pl_done = sem("pl_done")
        pv_done = sem("pv_done")
        o_copied = sem("o_copied")
        o_recip = sem("o_recip")
        o_summed = sem("o_summed")
        o_done = sem("o_done")
        to_psum = sem("to_psum")
        ot_hi = sem("ot_hi")
        ot_lo = sem("ot_lo")
        a_psum = sem("a_psum")
        p_st = sem("p_st")
        p_stat = sem("p_stat")
        p_eps = sem("p_eps")
        p_pow = sem("p_pow")
        p_nrm = sem("p_nrm")
        xres_in = [sem("xres_in0"), sem("xres_in1")]
        a_norm = sem("a_norm")
        x1_ready = sem("x1_ready")
        x1_out = [sem("x1_out0"), sem("x1_out1")]
        xn2_ready = sem("xn2_ready")
        xn_out = [sem("xn_out0"), sem("xn_out1")]
        tx_psum = sem("tx_psum")
        x2_hi = sem("x2_hi")
        x2_lo = sem("x2_lo")
        ff_psum = sem("ff_psum")
        ff_exp = sem("ff_exp")
        h_step = sem("h_step")
        h_ready = sem("h_ready")
        th_psum = sem("th_psum")
        ht_hi = sem("ht_hi")
        ht_lo = sem("ht_lo")
        dn_psum = sem("dn_psum")
        y_sb = sem("y_sb")
        y_out = [sem("y_out0"), sem("y_out1")]
        r_step = sem("r_step")
        r_carry = sem("r_carry")
        sel_ready = sem("sel_ready")
        wgt_ready = sem("wgt_ready")
        wgt_out = sem("wgt_out")
        slot_ready = sem("slot_ready")
        slot_copied = sem("slot_copied")
        tok_step = sem("tok_step")
        slot_put = sem("slot_put")
        slot_put_b = sem("slot_put_b")

        R = 4
        U = 8
        AHEAD = R - 1
        wup = view(stack, 0, R * 2 * C * FF).rearrange("p (n k c f) -> p n k c f", n=R, k=2, c=C)
        wdo = view(stack, R * 2 * C * FF, R * 2 * D).rearrange("p (n k d) -> p n k d", n=R, k=2)
        xg = view(xt_reg, 0, R * XW).rearrange("p (n d) -> p n d", n=R)
        xgT = view(xt_reg, R * XW, 2 * C * CAP).rearrange("p (n c s) -> p n c s", n=2, c=C)
        exg = view(xt_reg, R * XW + 2 * C * CAP, 2 * CAP).rearrange("p (k s) -> p k s", k=2)
        exh = view(xt_reg, R * XW + 2 * C * CAP + 2 * CAP, 2 * 2 * CAP).rearrange("p (n k s) -> p n k s", n=2, k=2)
        oe = view(o_reg, 0, 2 * D).rearrange("p (n d) -> p n d", n=2)
        slots = view(o_reg, 2 * D, E, U32)
        slot_c = view(o_reg, 2 * D + E, U, U32)
        idx_in = sem("idx_in")
        w_in = [sem(f"w_in{n}") for n in range(R)]
        idx_c = sem("idx_c")
        xg_in = [sem(f"xg_in{n}") for n in range(R)]
        xgt_psum = sem("xgt_psum")
        xgt_sb = sem("xgt_sb")
        up_psum = sem("up_psum")
        e_exp = sem("e_exp")
        e_step = sem("e_step")
        e_hid = sem("e_hid")
        eo_psum = sem("eo_psum")
        oe_ready = sem("oe_ready")
        oe_free = sem("oe_free")
        added = sem("added")
        all_added = sem("all_added")
        FT, FS = 4, 4
        fy = view(stack, 0, FS * FT * D).rearrange("p (n t d) -> p n t d", n=FS, t=FT)
        fx = view(stack, FS * FT * D, FS * FT * D).rearrange("p (n t d) -> p n t d", n=FS, t=FT)
        f_st = sb("f_st", FS * FT * 6)[:, :].rearrange("p (n t s) -> p n t s", n=FS, t=FT)
        f_mv = sb("f_mv", FS * FT * 2)[:, :].rearrange("p (n t s) -> p n t s", n=FS, t=FT)
        f_ve = sb("f_ve", FS * FT)[:, :].rearrange("p (n t) -> p n t", n=FS)
        f_rs = sb("f_rs", FS * FT)[:, :].rearrange("p (n t) -> p n t", n=FS)
        f_nm = sb("f_nm", FS * FT)[:, :].rearrange("p (n t) -> p n t", n=FS)
        f_pow = sem("f_pow")
        f_mr = sem("f_mr")
        f_in = [sem(f"f_in{n}") for n in range(FS)]
        f_stat = sem("f_stat")
        f_var = sem("f_var")
        f_eps = sem("f_eps")
        f_rstd = sem("f_rstd")
        f_norm = sem("f_norm")
        f_sum = sem("f_sum")
        f_out = [sem(f"f_out{n}") for n in range(FS)]
        NF = TOK // (FT * P)

        def experts_sync(sp):
            sp.wait_ge(slot_put, (NB + 1) * 16 * NT * K - 8 * NT * K)
            sp.wait_ge(slot_put_b, 8 * NT * K)
            sp.dma_start(slots[0:CAP, :], slot_d.rearrange("(s e) o -> s (e o)", e=E)).then_inc(idx_in, 16)
            with sp.Fori(0, E // R) as e0_turn:
                e0 = e0_turn * R
                for n in range(R):
                    sp.wait_ge(eo_psum, e0 + n + 1)
                    ups = lambda w: w[bass.ds(e0 + n, 1), :, :].rearrange("o (p c) f -> (o p) c f", c=C)
                    sp.dma_start(wup[:, n, 0, :, :], ups(w_gate)).then_inc(w_in[n], 16)
                    sp.dma_start(wup[:, n, 1, :, :], ups(w_up)).then_inc(w_in[n], 16)
                    down = w_down[bass.ds(e0 + n, 1), :, :].rearrange("o f d -> (o f) d")
                    sp.dma_start(wdo[:, n, 0, :], down[0:P, :]).then_inc(w_in[n], 16)
                    sp.dma_start(wdo[0:FR, n, 1, :], down[P:FF, :]).then_inc(w_in[n], 16)
            sp.wait_ge(all_added, 1)

            def final(i, n):
                rows = lambda d: d[bass.ds(i * (FT * P) + n * (FT * P), FT * P), :].rearrange("(t p) d -> p t d", p=P)
                sp.dma_start(fy[:, n, :, :], rows(y_d)).then_inc(f_in[n], 16)
                sp.dma_start(fx[:, n, :, :], rows(x1_d)).then_inc(f_in[n], 16)

            def store(i, n):
                sp.wait_ge(f_sum, i + n + 1)
                dst = outf[bass.ds(i * (FT * P) + n * (FT * P), FT * P), :].rearrange("(t p) d -> p t d", p=P)
                sp.dma_start(dst, fy[:, n, :, :]).then_inc(f_out[n], 16)

            for n in range(FS):
                final(0, n)
            with sp.Fori(0, NF // FS - 1) as i_turn:
                i = i_turn * FS
                for n in range(FS):
                    store(i, n)
                    sp.wait_ge(f_out[n], i * (16 // FS) + 16)
                    final(i + FS, n)
            for n in range(FS):
                store(NF - FS, n)
            for n in range(FS):
                sp.wait_ge(f_out[n], 16 * NF // FS)

        def experts_pool(pool):
            g = nc.gpsimd

            def gather(e, n):
                g.tensor_copy(slot_c[0:CAP, n:n + 1], slots[0:CAP, bass.ds(e, 1)]).then_inc(idx_c, 1)
                hold("pool", pool, idx_c, e + 1)
                g.indirect_dma_start(out=xg[0:CAP, n % R, :], out_offset=None, in_=xw_d,
                                     in_offset=bass.IndirectOffsetOnAxis(ap=slot_c[0:CAP, n:n + 1], axis=0),
                                     bounds_check=TOK + P - 1, oob_is_err=True).then_inc(xg_in[n % R], 16)

            def add(e, n, first=False):
                hold("pool", pool, oe_ready, e + 1)
                if not first:
                    hold("pool", pool, added, e * 16)
                    pool.sem_inc(oe_free, 1)
                g.indirect_dma_start(out=y_d, out_offset=bass.IndirectOffsetOnAxis(ap=slot_c[0:CAP, n:n + 1], axis=0),
                                     in_=oe[0:CAP, n % 2, :], in_offset=None, bounds_check=TOK + P - 1,
                                     oob_is_err=True, compute_op=ALU.add).then_inc(added, 16)

            hold("pool", pool, idx_in, 16)
            for n in range(2):
                hold("pool", pool, xn_out[n], NB * NT * 8)
                hold("pool", pool, y_out[n], NB * NT * 8)
            hold("pool", pool, wgt_out, NB * 32 + 16)
            hold("pool", pool, eo_psum, R)
            for n in range(AHEAD):
                gather(n, n)
            for n in range(U):
                gather(n + AHEAD, (n + AHEAD) % U)
                add(n, n, n == 0)
            with pool.Fori(1, E // U - 1) as e0_turn:
                e0 = e0_turn * U
                for n in range(U):
                    gather(e0 + n + AHEAD, (n + AHEAD) % U)
                    add(e0 + n, n)
            for n in range(U):
                if n + AHEAD < U:
                    gather(E - U + n + AHEAD, n + AHEAD)
                add(E - U + n, n)
            hold("pool", pool, added, E * 16)
            pool.sem_inc(all_added, 1)
            with pool.Fori(0, NF // FS) as i_turn:
                i = i_turn * FS
                for n in range(FS):
                    hold("pool", pool, f_var, i + n + 1)
                    g.tensor_scalar(f_ve[:, n, :], f_mv[:, n, :, 1], EPS, None, ALU.add).then_inc(f_eps, 1)
                    hold("pool", pool, f_eps, i + n + 1)
                    g.tensor_tensor(f_rs[:, n, :], f_ve[:, n, :], mhalf[:, 0:FT], ALU.pow).then_inc(f_pow, 1)
                    hold("pool", pool, f_pow, i + n + 1)
                    g.tensor_tensor(f_ve[:, n, :], f_mv[:, n, :, 0], f_rs[:, n, :], ALU.mult).then_inc(f_mr, 1)
                    hold("pool", pool, f_mr, i + n + 1)
                    g.tensor_scalar(f_nm[:, n, :], f_ve[:, n, :], -1.0, None, ALU.mult).then_inc(f_rstd, 1)

        def experts_act(act):
            a = nc.scalar
            with act.Fori(0, E // 2) as e0_turn:
                e0 = e0_turn * 2
                for n in range(2):
                    act.wait_ge(xgt_psum, e0 + n + 1)
                    a.activation(xgT[:, n, :, :], bank(n, C * CAP).rearrange("p (c s) -> p c s", c=C),
                                 ACT.Copy).then_inc(xgt_sb, 1)
                    act.wait_ge(up_psum, e0 + n + 1)
                    act.wait_ge(e_hid, e0 + n + 1)
                    a.activation(exg[:, 0, :], bank(2 + n, CAP), ACT.Exp, scale=-1.0).then_inc(e_exp, 1)
                    a.activation(exg[0:FR, 1, :], bank(2 + n, CAP, CAP)[0:FR], ACT.Exp, scale=-1.0).then_inc(e_exp, 1)

            with act.Fori(0, NF // FS) as i_turn:
                i = i_turn * FS
                for n in range(FS):
                    act.wait_ge(f_rstd, i + n + 1)
                    for t in range(FT):
                        ins = a.activation(fy[:, n, t, :], fy[:, n, t, :], ACT.Identity, bias=f_nm[:, n, t:t + 1],
                                           scale=f_rs[:, n, t:t + 1])
                    ins.then_inc(f_norm, 1)

        def experts_dve(dve):
            v = nc.vector
            dve.sem_inc(e_hid, 1)
            with dve.Fori(0, E // R) as e0_turn:
                e0 = e0_turn * R
                for n in range(R):
                    m = n % 2
                    dve.wait_ge(e_exp, (e0 + n) * 2 + 2)
                    blocks = [(0, P), (1, FR)]
                    k = (e0 + n) * 6
                    for i, (j, kp) in enumerate(blocks):
                        v.tensor_scalar(exg[0:kp, j, :], exg[0:kp, j, :], 1.0, None, ALU.add).then_inc(e_step, 1)
                    for i, (j, kp) in enumerate(blocks):
                        dve.wait_ge(e_step, k + i + 1)
                        v.reciprocal(exg[0:kp, j, :], exg[0:kp, j, :]).then_inc(e_step, 1)
                    for i, (j, kp) in enumerate(blocks):
                        dve.wait_ge(e_step, k + i + 3)
                        v.tensor_tensor(exh[0:kp, m, j, :], bank(2 + m, CAP, j * CAP)[0:kp], exg[0:kp, j, :],
                                        ALU.mult).then_inc(e_step, 1)
                    for i, (j, kp) in enumerate(blocks):
                        dve.wait_ge(e_step, k + i + 5)
                        ins = v.tensor_tensor(exh[0:kp, m, j, :], bank(2 + m, CAP, (2 + j) * CAP)[0:kp],
                                              exh[0:kp, m, j, :], ALU.mult)
                    ins.then_inc(e_hid, 1)
                    weigh(dve, e0 + n, n)

            def stats(i, n):
                dve.wait_ge(f_in[n], i * (32 // FS) + 32)
                for t in range(FT):
                    ins = v.bn_stats(f_st[:, n, t, :], fy[:, n, t, :])
                ins.then_inc(f_stat, 1)
                hold("dve", dve, f_stat, i + n + 1)
                for t in range(FT):
                    ins = v.bn_aggr(f_mv[:, n, t, :], f_st[:, n, t, :])
                ins.then_inc(f_var, 1)

            def residual(i, n):
                dve.wait_ge(f_norm, i + n + 1)
                v.tensor_tensor(fy[:, n, :, :], fy[:, n, :, :], fx[:, n, :, :], ALU.add).then_inc(f_sum, 1)

            stats(0, 0)
            stats(0, 1)
            with dve.Fori(0, NF // FS - 1) as i_turn:
                i = i_turn * FS
                for n in range(FS):
                    residual(i, n)
                    if n < FS - 2:
                        stats(i, n + 2)
                    else:
                        stats(i + FS, n + 2 - FS)
            for n in range(FS):
                residual(NF - FS, n)
                if n < FS - 2:
                    stats(NF - FS, n + 2)

        def weigh(dve, e, n):
            dve.wait_ge(eo_psum, R + e + 1)
            dve.wait_ge(oe_free, e + 1)
            nc.vector.tensor_scalar(oe[0:CAP, n % 2, :], bank(4 + n % 2)[0:CAP], xg[0:CAP, n, bass.ds(D + e, 1)], None,
                                    ALU.mult).then_inc(oe_ready, 1)

        def experts_pe(pe):
            mm = nc.tensor.matmul
            pe.drain().then_inc(eo_psum, R)

            def turn(e, n, round_):
                pe.wait_ge(xg_in[n], round_)
                for c in range(C):
                    ins = nc.tensor.transpose(bank(n % 2, CAP, c * CAP), xg[0:CAP, n, c:D:C], ident[0:CAP, 0:CAP])
                ins.then_inc(xgt_psum, 1)

            def up(e, n, round_):
                pe.wait_ge(xgt_sb, e + 1)
                pe.wait_ge(w_in[n], round_)
                for k in range(2):
                    for j, kp in ((0, P), (1, FR)):
                        for c in range(C):
                            ins = mm(bank(2 + n % 2, CAP, (2 * k + j) * CAP)[0:kp], wup[:, n, k, c, j * P:j * P + kp],
                                     xgT[:, n % 2, c, :], start=c == 0, stop=c == C - 1)
                ins.then_inc(up_psum, 1)

            def down(e, n):
                pe.wait_ge(e_hid, e + 2)
                mm(bank(4 + n % 2)[0:CAP], exh[:, n % 2, 0, :], wdo[:, n, 0, :], start=True, stop=False)
                mm(bank(4 + n % 2)[0:CAP], exh[0:FR, n % 2, 1, :], wdo[0:FR, n, 1, :], start=False,
                   stop=True).then_inc(eo_psum, 1)

            def steady(j, i, q):
                turn(j + 2, (i + 2) % R, q * 4 + (16 if i + 2 < R else 32))
                up(j + 1, (i + 1) % R, q * 16 + (64 if i + 1 < R else 128))
                down(j, i)

            turn(0, 0, 16)
            turn(1, 1, 16)
            up(0, 0, 64)
            with pe.Fori(0, (E - R) // R) as e0_turn:
                e0 = e0_turn * R
                for i in range(R):
                    steady(e0 + i, i, e0)
            for i in range(R - 2):
                steady(E - R + i, i, E - R)
            up(E - 1, R - 1, (E // R) * 64)
            down(E - 2, R - 2)
            down(E - 1, R - 1)

        N_CONST = 16
        V_CONST = 8

        block = ctx.enter_context(nc.Block())

        w32 = view(stack, 0, C * 3 * D).rearrange("p (c o) -> p c o", c=C)
        wo32 = view(stack, C * 3 * D, C * D).rearrange("p (c o) -> p c o", c=C)
        wff32 = view(stack, C * 4 * D, C * FW).rearrange("p (c o) -> p c o", c=C)
        wdn32 = view(stack, C * 4 * D + C * FW, 2 * D).rearrange("p (c o) -> p c o", c=2)
        SPLITS = [(w32, wqkv), (wo32, wo), (wff32, wff), (wdn32[:, 0, :], wdn[:, :, 0, :]),
                  (wdn32[0:FR, 1, :], wdn[0:FR, :, 1, :])]
        STK = 16 * 3 * HPC
        RS = 90
        H_SCALE = S_H / (S_X * S_W) ** 2

        def loop_over_heads(eng, b, step, wait_rows, more):
            ln = (lambda t: t) if more else (lambda t: None)
            L = 2 if more else 0
            project = {0: {1: (2, 0, 0), 4: (2, 0, 1)}, 1: {3: (2, 1, 0)}, 2: {0: (2, 1, 1)},
                       3: {4: (3, 0, 0)}, 4: {3: (3, 0, 1)}, 5: {3: (3, 1, 0)}, 6: {0: (3, 1, 1)}}
            t = tiles_at(b, 0)
            for h in range(9):
                if h in (HPC, 2 * HPC):
                    wait_rows(b, h // HPC)
                step(b, h, t, s=h + LEAD, sc=(h + LEAD) % HPC, a=project.get(h, {}),
                     m=(h + 1) // HPC if h % HPC == 3 else None)
            at = 9 * N_S + 8 + 2 * 2
            with eng.Fori(0, 2) as q:
                step(b, q + 9, tiles_at(b, q * (N_S + L) + at), s=q + 9 + LEAD, sc=q + 2, ln=ln(q))
            at += 2 * (N_S + L)
            step(b, 11, tiles_at(b, at), ln=ln(2), m=3)
            wait_rows(b, 3)
            with eng.Fori(0, 4) as q:
                step(b, q + 12, tiles_at(b, q * L + at + 2 + L), ln=ln(q + 3))

        def tiles_at(b, at):
            return Tiles(b * N_SEQ + (PRO + N_OPEN + at))

        def tiles_after(b, more):
            if isinstance(b, int) and b < 0:
                return Tiles(PRO)
            return tiles_at(b, N_LOOP if more else N_LOOP - 2 * (NT - 1))

        @block.sync
        def _(sp):
            def load_x(n):
                sp.wait_ge(xl_ready, n + 1)
                sp.dma_start(xl_in[:, :], xf[bass.ds(n * P, P), :]).then_inc(x_in, 16)

            def stack_up(b, g, k, n):
                sp.wait_ge(aux_free, n + 1)
                for r, part in enumerate(((0, 0, 1), (0, 1, 0))[k]):
                    for j in range(HPC):
                        sp.dma_start((stq, stk)[k][r * DH:(r + 1) * DH, bass.ds(g * HPC + j, 1), :],
                                     stg[j * DH:(j + 1) * DH, k, part:part + 1, :]).then_inc(stacked[k], 16)

            def rows_up(b, g, n):
                sp.wait_ge(aux_free, n + 2)
                for l in range(2):
                    dst = stq[3 * DH + l:3 * DH + l + 1, bass.ds(g * HPC, HPC), :]
                    dst = dst.rearrange("o h (i q) -> o (h i) q", q=P)
                    sp.dma_start(dst, mrow[0:HPC * NT, l, :]).then_inc(m_rows, 16)

            load_x(0)
            ld = lambda d, s: sp.dma_start(d, s).then_inc(s_wld, 16)
            ld(w32, w_qkv_t.rearrange("(c p) o -> p c o", p=P))
            ld(wo32, w_out_t.rearrange("(c p) o -> p c o", p=P))
            ld(wff32[:, :, 0:FF], ws_gate.rearrange("(c p) o -> p c o", p=P))
            ld(wff32[:, :, FF:FF + E], gate_w.rearrange("(c p) o -> p c o", p=P))
            ld(wff32[:, :, FF + E:FW], ws_up.rearrange("(c p) o -> p c o", p=P))
            ld(wdn32[:, 0, :], ws_down[0:P, :])
            ld(wdn32[0:FR, 1, :], ws_down[P:FF, :])
            ld(bias_b[:, :], bias.partition_broadcast(P))
            sp.wait_ge(s_const, N_CONST)
            sp.dma_start(xw_d[TOK:TOK + P, :], zeros_row).then_inc(s_init, 16)
            sp.dma_start(y_d[TOK:TOK + P, :], zeros_row[:, 0:D]).then_inc(wgt_out, 16)
            sp.dma_start(slot_d.rearrange("(s e) o -> s (e o)", e=E), slot_init[0:CAP, :]).then_inc(s_init, 16)

            def step(b, h, tiles, s=None, sc=None, a={}, ln=None, m=None):
                if ln is not None:
                    load_x((b + 1) * NT + ln)
                n = tiles.first + tiles.n
                tiles.take((N_S if s is not None else 0) + len(a) + 2 * (m is not None) + 2 * (ln is not None))
                for k, gi in enumerate(a):
                    g, qk, half = a[gi]
                    if half == 1:
                        stack_up(b, g, qk, n + 2 * (gi + 1) + k)
                if m is not None:
                    rows_up(b, m, n + 6 if s is not None else n)

            def beside(b, items, tiles):
                for kind, *what in items:
                    if kind == "in order":
                        continue
                    n, _ = tiles.take(2 if kind in ("ln", "rows") else 1)
                    if kind == "a" and what[2] == 1:
                        stack_up(b, what[0], what[1], n)
                    if kind == "rows":
                        if isinstance(b, int) and b == 0:
                            sp.wait_ge(s_rows, 3)
                        rows_up(b, 0, n)

            def after(b, post, more):
                tiles = tiles_after(b, more)
                row = lambda t: bass.ds(b * SEQ + t * P, P)
                if more:
                    load_x((b + 1) * NT + NT - 1)
                if post:
                    sp.wait_ge(pv_done, NG * (b * NH + NH))
                    for t in range(2):
                        sp.dma_start(x1[:, t, :], xf[row(t), :]).then_inc(xres_in[t], 16)
                for s in range(TURNS):
                    if more:
                        for part in BESIDE[s]:
                            beside(b + 1, part, tiles)
                    if post and s < NT:
                        sp.wait_ge(x1_ready, b * NT + s + 1)
                        sp.dma_start(x1_d[row(s), :], x1[:, s % 2, :]).then_inc(x1_out[s % 2], 16)
                        sp.wait_ge(xn2_ready, b * NT + s + 1)
                        sp.dma_start(xw_d[row(s), 0:D], xn[:, s % 2, :]).then_inc(xn_out[s % 2], 16)
                        if s + 2 < NT:
                            sp.wait_ge(x1_out[s % 2], (b * (NT // 2) + s // 2 + 1) * 16)
                            sp.dma_start(x1[:, s % 2, :], xf[row(s + 2), :]).then_inc(xres_in[s % 2], 16)
                    if post and s >= 3:
                        sp.wait_ge(y_sb, b * NT + s - 3 + 1)
                        sp.dma_start(y_d[row(s - 3), :], ysh[:, (s - 3) % 2, :]).then_inc(y_out[(s - 3) % 2], 16)
                    if post and s == HT + 3:
                        tiles.take(2)
                    if post and s in (HT + 3, TURNS - 1):
                        hf = int(s == TURNS - 1)
                        sp.wait_ge(wgt_ready, b * 2 + hf + 1)
                        dst = xw_d[bass.ds(b * SEQ + hf * HALF, HALF), D:XW].rearrange("(t p) e -> p t e", p=P)
                        sp.dma_start(dst, wgt[hf]).then_inc(wgt_out, 16)

            for t in range(1, NT - 1):
                load_x(t)
            after(-1, False, True)
            with sp.Fori(0, NB - 1) as b:
                loop_over_heads(sp, b, step, lambda b, g: None, True)
                after(b, True, True)
            loop_over_heads(sp, NB - 1, step, lambda b, g: None, False)
            after(NB - 1, True, False)
            experts_sync(sp)

        @block.gpsimd
        def _(pool):
            g = nc.gpsimd
            pool.sem_inc(xl_ready, 1)
            inc = lambda i: i.then_inc(s_const, 1)
            inc(g.memset(ident[:, :], 0.0))
            inc(g.memset(ident_b[:, :], 0.0))
            inc(g.memset(mask_qk[:, :], 0.0))
            inc(g.memset(mask_kq[:, :], 0.0))
            inc(g.memset(earlier[:, :], 1.0))
            inc(g.memset(ones_b[:, :], 1.0))
            inc(g.memset(mhalf[:, :], -0.5))
            inc(g.memset(zeros_row, 0.0))
            pool.wait_ge(s_const, 8)
            aff = lambda t, cmp, fill, base, cm, st: inc(g.affine_select(
                out=t[:, :], in_=t[:, :], compare_op=cmp, fill=fill, base=base, pattern=[[st, P]], channel_multiplier=cm))
            aff(ident, ALU.not_equal, 1.0, 0, 1, -1)
            aff(ident_b, ALU.not_equal, 1.0, 0, 1, -1)
            aff(mask_qk, ALU.is_ge, -BIG, 0, 1, -1)
            aff(mask_kq, ALU.is_ge, -BIG, 0, -1, 1)
            aff(earlier, ALU.is_ge, 0.0, -1, -1, 1)
            inc(g.iota(slot_init[:, :], pattern=[[0, E]], base=TOK, channel_multiplier=1))
            inc(g.iota(tok_c[:, :], pattern=[[P, NT], [0, K]], base=0, channel_multiplier=1))
            inc(g.iota(cols_i[:, :], pattern=[[1, E]], base=0, channel_multiplier=0))

            pool.wait_ge(s_const, N_CONST)
            pool.wait_ge(s_vconst, 8)
            pool.wait_ge(s_init, 32)
            pool.sem_inc(o_done, 2)
            pool.sem_inc(slot_ready, 2)
            pool.sem_inc(oe_free, 2)

            def norm(stat, n, var, mean, r, eps, s_eps, s_pow, s_nrm):
                hold("pool", pool, stat, n + 1)
                g.tensor_scalar(r[:, 0:1], var, eps, None, ALU.add).then_inc(s_eps, 1)
                hold("pool", pool, s_eps, n + 1)
                g.tensor_tensor(r[:, 1:2], r[:, 0:1], mhalf[:, 0:1], ALU.pow).then_inc(s_pow, 1)
                hold("pool", pool, s_pow, n + 1)
                g.tensor_scalar(r[:, 2:3], mean, r[:, 1:2], -1.0, ALU.mult, ALU.mult).then_inc(s_nrm, 1)

            def first_norm(n):
                norm(ln_stat, n, lmv[:, 1:2], lmv[:, 0:1], lnr, EPS, ln_eps, ln_pow, ln_nrm)

            def later_norm(n, k):
                c = k % 4
                eps = EPS * (S_V * S_W) ** 2 if k % 2 == 0 else EPS
                norm(p_stat, n, mv2[:, c, 1:2], mv2[:, c, 0:1], nr2[:, c, :], eps, p_eps, p_pow, p_nrm)

            def attn_out(n, h, half):
                hold("pool", pool, o_copied, n + 1)
                g.tensor_tensor(osum[:, half, :, :], osb[:, half, :, 0:DH], osb[:, half, :, DH + 1:2 * DH + 1],
                                ALU.add).then_inc(o_summed, 1)
                pool.wait_ge(o_recip, n + 1)
                hold("pool", pool, o_summed, n + 1)
                g.tensor_tensor(o_sb[:, half * HT:(half + 1) * HT, bass.ds(h * DH, DH)], osum[:, half, :, :],
                                orec[:, half, :, :].to_broadcast((P, HT, DH)), ALU.mult).then_inc(o_done, 1)

            def put_slots(n, c, p=0):
                k = K // 2
                g.tensor_copy(slot_3[:, p * k:(p + 1) * k], slot_i[:, bass.ds(c, k)]).then_inc(slot_copied, 1)
                g.tensor_copy(tok_3[:, p * k:(p + 1) * k], tok_i[:, bass.ds(c, k)]).then_inc(slot_copied, 1)
                hold("pool", pool, slot_copied, 2 * n + 2)
                for j in range(k):
                    g.indirect_dma_start(
                        out=slot_d, out_offset=bass.IndirectOffsetOnAxis(ap=slot_3[:, p * k + j:p * k + j + 1], axis=0),
                        in_=tok_3[:, p * k + j:p * k + j + 1], in_offset=None, bounds_check=CAP * E - 1,
                        oob_is_err=False).then_inc(slot_put_b if p else slot_put, 16)

            def step(b, h, tiles, s=None, sc=None, a={}, ln=None, m=None):
                n = b * NH + h
                put_slots(n, h * (K // 2))
                if ln is not None:
                    first_norm((b + 1) * NT + ln)
                if not (isinstance(h, int) and h == 0):
                    attn_out(2 * n - 1, h - 1, 1)
                attn_out(2 * n, h, 0)
                hold("pool", pool, slot_put, n * (8 * K) + 8 * K)
                if isinstance(h, int) and h == 0:
                    hold("pool", pool, slot_ready, b * 2 + 2)

            def count_before(b, hf):
                hold("pool", pool, sel_ready, b * 2 + hf + 1)
                for t in range(HT):
                    n = b * (2 * NT) + 2 * (hf * HT + t)
                    g.tensor_copy(before_b[hf][:, t, :], carry[:, :]).then_inc(r_carry, 1)
                    hold("pool", pool, r_carry, n + 1)
                    g.tensor_tensor(carry[:, :], carry[:, :], sel[hf][:, t, :], ALU.add).then_inc(r_carry, 1)
                    hold("pool", pool, r_carry, n + 2)

            def sequence(b, more):
                hold("pool", pool, slot_ready, b * 2 + 1)
                hold("pool", pool, wgt_out, b * 32 + 16)
                loop_over_heads(pool, b, step, lambda b, g: None, more)
                attn_out(2 * (b * NH + NH) - 1, NH - 1, 1)
                if more:
                    first_norm((b + 1) * NT + NT - 1)
                for k in range(2 * NT):
                    if k == 2 * (HT + 3):
                        count_before(b, 0)
                    later_norm(b * (2 * NT) + k, k)
                count_before(b, 1)
                g.tensor_scalar(tok_f[:, :], tok_f[:, :], float(SEQ), None, ALU.add).then_inc(tok_step, 1)
                hold("pool", pool, tok_step, 2 * b + 1)
                g.tensor_copy(tok_i[:, :], tok_f[:, :]).then_inc(tok_step, 1)
                hold("pool", pool, tok_step, 2 * b + 2)

            for t in range(NT):
                first_norm(t)
            word = lambda value: float(np.array([value, value], np.float16).view(np.float32)[0])
            pool.wait_ge(s_wlo, len(SPLITS))
            pool.wait_ge(ln_nrm, NT)
            g.memset(stack[3 * DH:P, :], 0.0).then_inc(s_rows, 1)
            pool.wait_ge(s_rows, 1)
            g.memset(stack[3 * DH:3 * DH + 2, NH * SEQ // 2:NH * SEQ], word(-1.0)).then_inc(s_rows, 1)
            pool.wait_ge(s_rows, 2)
            g.memset(stack[3 * DH:3 * DH + 1, NH * SEQ // 2:NH * SEQ], word(M_HI)).then_inc(s_rows, 1)
            pool.wait_ge(s_rows, 3)
            with pool.Fori(0, NB - 1) as b:
                sequence(b, True)
            sequence(NB - 1, False)
            hold("pool", pool, slot_ready, NB * 2 + 2)
            put_slots(NB * NH, 0)
            put_slots(NB * NH + 1, K // 2, 1)
            with pool.Fori(1, NH // 2) as h2:
                for p in range(2):
                    if p == 0:
                        hold("pool", pool, slot_put, h2 * (8 * K) + NB * NH * 8 * K)
                    else:
                        hold("pool", pool, slot_put_b, h2 * (8 * K))
                    put_slots(h2 * 2 + p + NB * NH, h2 * K + p * (K // 2), p)
            experts_pool(pool)

        @block.scalar
        def _(act):
            a_ = nc.scalar
            copy = lambda o, i, scale=1.0: a_.activation(o, i, ACT.Copy, scale=scale)
            def ln_apply(n):
                act.wait_ge(ln_nrm, n + 1)
                a_.activation(xl[:, :], xl_in[:, :], ACT.Identity, bias=lnr[:, 2:3],
                              scale=lnr[:, 1:2]).then_inc(xl_ready, 1)

            def ln_hi(t, tiles):
                n, k = tiles.take(2)
                act.wait_ge(aux_full, n + 2)
                copy(xT[:, 0, :, bass.ds(t * P, P)], aux(k).rearrange("p (c s) -> p c s", c=C), S_X).then_inc(xt_hi, 1)

            def v_part(t, tiles):
                n, k = tiles.take()
                act.wait_ge(aux_full, n + 1)
                copy(vv[:, t, :, 0:DH], aux(k).rearrange("p (h d) -> p h d", h=NH), S_V / (S_X * S_W)).then_inc(v_hi, 1)

            def a_part(b, g, qk, half, tiles):
                n, k = tiles.take()
                act.wait_ge(aux_full, n + 1)
                if half == 0 and not (isinstance(b, int) and b == 0 and g == 0):
                    act.wait_ge(stacked[qk], (b * (NH // HPC) + g) * STK)
                copy(stg[:, qk, 0, half * HALF:(half + 1) * HALF], aux(k), S_QK / (S_X * S_W)).then_inc(a_hi, 1)

            def maxima(b, g, tiles):
                n, k = tiles.take(2)
                act.wait_ge(aux_full, n + 2)
                if not (isinstance(b, int) and b == 0 and isinstance(g, int) and g == 0):
                    act.wait_ge(m_rows, (b * (NH // HPC) + g) * 32)
                copy(mrow[0:HPC * NT, 0, :], aux(k, P)[0:HPC * NT], -1.0 / M_HI).then_inc(m_hi, 1)

            def exp(n, gi, w, fresh):
                act.wait_ge(st_psum, n + 1)
                if not (fresh and gi < 3):
                    act.wait_ge(pl_done, n - 2)
                a_.activation(p32[:, gi % 3, 0:w], bank(2 * (gi % 2), w), ACT.Exp, bias=ln_sp[:, 0:1],
                              scale=SM_SCALE).then_inc(exp_done, 1)

            def prob_hi(n, gi, w, fresh):
                act.wait_ge(exp_done, n + 1)
                if not (fresh and gi < 3):
                    act.wait_ge(pv_done, n - 2)
                copy(phl[:, gi % 3, 0, 0:w], p32[:, gi % 3, 0:w]).then_inc(ph_done, 1)

            def copy_out(b, h, half):
                n = 2 * (b * NH + h) + half
                act.wait_ge(pv_done, NG * (b * NH + h) + (NG if half else 2))
                act.wait_ge(o_done, n + 1)
                copy(osb[:, half, :, 0:2 * DH + 1], o_bank(half)).then_inc(o_copied, 1)

            def step(b, h, tiles, s=None, sc=None, a={}, ln=None, m=None):
                fresh = isinstance(h, int) and h == 0
                for gi in range(NG):
                    n = NG * (b * NH + h) + gi
                    exp(n, gi, group_blocks(gi)[1], fresh)
                    if not (fresh and gi == 0) and not (s is None and gi - 1 in HI_BY_DVE):
                        prob_hi(n - 1, (gi - 1) % NG, group_blocks((gi - 1) % NG)[1], fresh and gi > 0)
                    if gi == 3 and not fresh:
                        copy_out(b, h - 1, 1)
                    if gi == 5:
                        copy_out(b, h, 0)
                    if s is not None:
                        tiles.take(2)
                    if gi in a:
                        a_part(b, *a[gi], tiles)
                    if ln is not None and gi == 3:
                        ln_apply((b + 1) * NT + ln)
                    if m is not None and gi == 2:
                        maxima(b, m, tiles)
                    if ln is not None and gi == 5:
                        ln_hi(ln, tiles)

            def beside(b, items, tiles):
                for kind, *what in items:
                    if kind == "ln":
                        ln_hi(NT - 1, tiles)
                    elif kind == "v":
                        v_part(what[0], tiles)
                    elif kind == "a":
                        a_part(b, *what, tiles)
                    elif kind == "s":
                        tiles.take()
                    elif kind == "rows":
                        maxima(b, 0, tiles)

            def after(b, post, more):
                tiles = tiles_after(b, more)
                if post:
                    n = NG * (b * NH + NH)
                    prob_hi(n - 1, NG - 1, group_blocks(NG - 1)[1], False)
                    copy_out(b, NH - 1, 1)
                if more:
                    ln_apply((b + 1) * NT + NT - 1)
                for s in range(TURNS):
                    u, r = b * NT + s - 2, b * NT + s - 3
                    if post and 2 <= s < NT + 2:
                        act.wait_ge(tx_psum, u + 1)
                        if s >= 4:
                            act.wait_ge(ff_psum, u - 1)
                        copy(x2T[:, s % 2, 0, :], bank(TX), S_X).then_inc(x2_hi, 1)
                    if post and s < NT:
                        act.wait_ge(to_psum, b * NT + s + 1)
                        if s >= 2:
                            act.wait_ge(a_psum, b * NT + s - 1)
                        copy(oT[:, s % 2, 0, :], bank(TO)).then_inc(ot_hi, 1)
                    if more:
                        beside(b + 1, BESIDE[s][0], tiles)
                    if post and 1 <= s < NT + 1:
                        k = 2 * s - 1
                        act.wait_ge(p_nrm, b * (2 * NT) + k + 1)
                        a_.activation(xn[:, (s - 1) % 2, :], x1[:, (s - 1) % 2, :], ACT.Identity,
                                      bias=nr2[:, k % 4, 2:3], scale=nr2[:, k % 4, 1:2]).then_inc(xn2_ready, 1)
                    if post and 2 <= s < NT + 2:
                        act.wait_ge(ff_psum, u + 1)
                        if s >= 3:
                            act.wait_ge(h_ready, u)
                        a_.activation(gex, bank(FU, FF + E), ACT.Exp, scale=-1.0 / (S_X * S_W)).then_inc(ff_exp, 1)
                    if post and s >= 3:
                        act.wait_ge(dn_psum, r + 1)
                        if s >= 5:
                            act.wait_ge(y_out[(s - 3) % 2], (b * (NT // 2) + (s - 3) // 2) * 16)
                        copy(ysh[:, (s - 3) % 2, :], bank(DN), 1.0 / (S_H * S_W)).then_inc(y_sb, 1)
                    if post and s < NT:
                        k, c = 2 * s, (2 * s) % 4
                        act.wait_ge(p_nrm, b * (2 * NT) + k + 1)
                        if s >= 2:
                            act.wait_ge(xn_out[s % 2], (b * (NT // 2) + s // 2) * 16)
                            act.wait_ge(tx_psum, b * NT + s - 1)
                        a_.activation(xn[:, s % 2, :], bank(AO), ACT.Identity, bias=nr2[:, c, 2:3],
                                      scale=nr2[:, c, 1:2]).then_inc(a_norm, 1)
                    if more:
                        beside(b + 1, BESIDE[s][1], tiles)
                    if post and 2 <= s < NT + 2:
                        act.wait_ge(th_psum, u + 1)
                        if s >= 3:
                            act.wait_ge(dn_psum, u)
                        copy(hT[:, 0, 0, :], bank(TH, P), H_SCALE).then_inc(ht_hi, 1)
                        copy(hT[0:FR, 0, 1, :], bank(TH, P, P)[0:FR], H_SCALE).then_inc(ht_hi, 1)
                    if more:
                        beside(b + 1, BESIDE[s][2], tiles)
                    if post and s == HT + 3:
                        tiles.take(2)
                if post:
                    for n in range(2):
                        act.wait_ge(y_out[n], (b * (NT // 2) + NT // 2) * 16)
                        act.wait_ge(x1_out[n], (b * (NT // 2) + NT // 2) * 16)
                        act.wait_ge(xn_out[n], (b * (NT // 2) + NT // 2) * 16)

            act.wait_ge(s_init, 32)
            act.wait_ge(wgt_out, 16)
            tiles = Tiles(0)
            for t in range(NT - 1):
                ln_apply(t)
                ln_hi(t, tiles)
                if t < len(SPLITS):
                    src, dst = SPLITS[t]
                    act.wait_ge(s_wld, 16 * 8)
                    copy(dst[:, 0], src, S_W).then_inc(s_whi, 1)
            act.wait_ge(s_vconst, V_CONST)
            after(-1, False, True)
            with act.Fori(0, NB - 1) as b:
                loop_over_heads(act, b, step, lambda b, g: None, True)
                after(b, True, True)
            loop_over_heads(act, NB - 1, step, lambda b, g: None, False)
            after(NB - 1, True, False)
            experts_act(act)

        def routing(dve, b, k):
            v = nc.vector

            def step(ins):
                k[0] += 1
                ins.then_inc(r_step, 1)

            def link(ins):
                step(ins)
                hold("dve", dve, r_step, b * RS + k[0])

            def best_groups(hf):
                link(v.tensor_tensor(scb[hf], sc_t[:, hf * HT:(hf + 1) * HT, :],
                                     bias_b[:, :].rearrange("p (o e) -> p o e", o=1).to_broadcast((P, HT, E)), ALU.add))
                gx = scb[hf].rearrange("p t (g m) -> p (t g) m", g=G)
                hi1 = cand[hf].rearrange("p t (g m) -> p (t g) m", g=G)[:, :, 0:4]
                lo1 = cand[hf].rearrange("p t (g m) -> p (t g) m", g=G)[:, :, 4:8]
                step(v.tensor_tensor(hi1, gx[:, :, 0:4], gx[:, :, 4:8], ALU.max))
                link(v.tensor_tensor(lo1, gx[:, :, 0:4], gx[:, :, 4:8], ALU.min))
                rg = rest[hf].rearrange("p t (g m) -> p (t g) m", g=G)
                step(v.tensor_tensor(rg[:, :, 0:2], hi1[:, :, 0:2], hi1[:, :, 2:4], ALU.max))
                step(v.tensor_tensor(rg[:, :, 2:4], hi1[:, :, 0:2], hi1[:, :, 2:4], ALU.min))
                link(v.tensor_tensor(rg[:, :, 4:6], lo1[:, :, 0:2], lo1[:, :, 2:4], ALU.max))
                link(v.tensor_tensor(rg[:, :, 6:8], rg[:, :, 2:4], rg[:, :, 4:6], ALU.max))
                wg = wgt[hf].rearrange("p t (g m) -> p (t g) m", g=G)
                step(v.tensor_tensor(wg[:, :, 0:1], rg[:, :, 0:1], rg[:, :, 1:2], ALU.max))
                step(v.tensor_tensor(wg[:, :, 1:2], rg[:, :, 0:1], rg[:, :, 1:2], ALU.min))
                link(v.tensor_tensor(wg[:, :, 2:3], rg[:, :, 6:7], rg[:, :, 7:8], ALU.max))
                link(v.tensor_tensor(wg[:, :, 3:4], wg[:, :, 1:2], wg[:, :, 2:3], ALU.max))
                wt = wgt[hf].rearrange("p t (g m) -> p t g m", g=G)
                link(v.tensor_tensor(gpad[:, :, 0:G], wt[:, :, :, 0], wt[:, :, :, 3], ALU.add))
                for t in range(HT):
                    step(v.max(top8[:, t, :], gpad[:, t, :]))
                hold("dve", dve, r_step, b * RS + k[0])
                link(v.memset(top8[:, :, KG:8], -BIG))
                for t in range(HT):
                    step(v.match_replace(gout[:, t, :], top8[:, t, :], gpad[:, t, :], -BIG))
                hold("dve", dve, r_step, b * RS + k[0])
                gm = gmask[:, :].rearrange("p (t g) -> p t g", t=HT)
                link(v.tensor_tensor(gm, gout[:, :, 0:G], gpad[:, :, 0:G], ALU.not_equal))
                link(v.tensor_scalar(gneg[:, :], gmask[:, :], BIG, BIG, ALU.mult, ALU.subtract))
                cg = cand[hf].rearrange("p t (g m) -> p (t g) m", g=G)
                by_group = lambda t: t[:, :].rearrange("p (n o) -> p n o", o=1).to_broadcast((P, HT * G, 8))
                link(v.tensor_tensor(cg, gx, by_group(gmask), ALU.mult))
                link(v.tensor_tensor(cg, cg, by_group(gneg), ALU.add))

            def best_experts(hf):
                for t in range(HT):
                    step(v.max(top8[:, t, :], cand[hf][:, t, :]))
                hold("dve", dve, r_step, b * RS + k[0])
                link(v.memset(top8[:, :, K:8], -BIG))
                for t in range(HT):
                    step(v.match_replace(rest[hf][:, t, :], top8[:, t, :], cand[hf][:, t, :], -BIG))
                hold("dve", dve, r_step, b * RS + k[0])
                link(v.tensor_tensor(sel[hf], rest[hf], cand[hf], ALU.not_equal))
                step(v.tensor_copy(sel_b[hf], sel[hf]))
                v.tensor_tensor(wgt[hf], sc_t[:, hf * HT:(hf + 1) * HT, :], sel[hf], ALU.mult).then_inc(sel_ready, 1)
                dve.wait_ge(sel_ready, b * 2 + hf + 1)
                link(v.reduce_sum(wsum[:, :, :], wgt[hf], AX_X))
                link(v.reciprocal(wsum[:, :, :], wsum[:, :, :]))
                v.scalar_tensor_tensor(out=wgt[hf], in0=wgt[hf], scalar=ROUTE_SCALE,
                                       in1=wsum[:, :, :].to_broadcast((P, HT, E)), op0=ALU.mult,
                                       op1=ALU.mult).then_inc(wgt_ready, 1)

            def to_slots(hf, tiles):
                n, bk = tiles.take(2)
                dve.wait_ge(aux_full, n + 2)
                pos = aux(bk, HT * E).rearrange("p (t e) -> p t e", t=HT)
                step(v.scalar_tensor_tensor(out=rest[hf], in0=pos, scalar=float(CAP), in1=sel[hf], op0=ALU.is_lt,
                                            op1=ALU.mult))
                v.scalar_tensor_tensor(out=neg[hf], in0=pos, scalar=-float(E),
                                       in1=slot_e[:, :].rearrange("p (o e) -> p o e", o=1).to_broadcast((P, HT, E)),
                                       op0=ALU.mult, op1=ALU.subtract).then_inc(aux_free, 2)
                dve.wait_ge(aux_free, n + 2)
                dve.wait_ge(r_step, b * RS + k[0])
                link(v.scalar_tensor_tensor(out=neg[hf], in0=neg[hf], scalar=NO_SLOT, in1=rest[hf], op0=ALU.add,
                                            op1=ALU.mult))
                link(v.tensor_scalar(neg[hf], neg[hf], -NO_SLOT, None, ALU.add))
                for t in range(HT):
                    step(v.max(top8[:, t, :], neg[hf][:, t, :]))
                hold("dve", dve, r_step, b * RS + k[0])
                dve.wait_ge(slot_copied, b * (2 * NH) + 2 * NH)
                mine = slot_i[:, hf * HT * K:(hf + 1) * HT * K].rearrange("p (t k) -> p t k", t=HT)
                v.tensor_scalar(mine, top8[:, :, 0:K], -1.0, None, ALU.mult).then_inc(slot_ready, 1)

            return best_groups, best_experts, to_slots


        @block.vector
        def _(dve):
            v = nc.vector
            vi = lambda i: i.then_inc(s_vconst, 1)
            vi(v.memset(ln_sp[:, :], LN_SP))
            vi(v.memset(vv[:, :, :, DH:DH + 1], 1.0))
            vi(v.memset(gpad[:, :, :], -BIG))
            vi(v.memset(carry[:, :], 0.0))
            vi(v.memset(slot_i[:, :], int(NO_SLOT)))
            vi(v.memset(tok_i[:, :], 0))
            dve.wait_ge(s_const, N_CONST)
            vi(v.tensor_copy(slot_e[:, :], cols_i[:, :]))
            vi(v.tensor_scalar(tok_f[:, :], tok_c[:, :], -float(SEQ), None, ALU.add))

            def rest_of(out, psum, scale, hi):
                return v.scalar_tensor_tensor(out=out, in0=psum, scalar=scale, in1=hi, op0=ALU.mult, op1=ALU.subtract)

            def ln_stats(n):
                dve.wait_ge(x_in, n * 16 + 16)
                v.bn_stats(lst[:, :], xl_in[:, :]).then_inc(ln_st, 1)
                hold("dve", dve, ln_st, n + 1)
                v.bn_aggr(lmv[:, :], lst[:, :]).then_inc(ln_stat, 1)

            def ln_lo(n, t, tiles):
                _, k = tiles.take(2)
                dve.wait_ge(xt_hi, n + 1)
                cols = bass.ds(t * P, P)
                rest_of(xT[:, 1, :, cols], aux(k).rearrange("p (c s) -> p c s", c=C), S_X,
                        xT[:, 0, :, cols]).then_inc(aux_free, 2)

            def v_part(n, t, tiles):
                _, k = tiles.take()
                dve.wait_ge(v_hi, n + 1)
                rest_of(vv[:, t, :, DH + 1:2 * DH + 1], aux(k).rearrange("p (h d) -> p h d", h=NH), S_V / (S_X * S_W),
                        vv[:, t, :, 0:DH]).then_inc(aux_free, 1)

            def a_part(b, g, qk, half, tiles):
                _, k = tiles.take()
                dve.wait_ge(a_hi, (b * NT + g * 2 + qk) * 2 + half + 1)
                cols = slice(half * HALF, (half + 1) * HALF)
                rest_of(stg[:, qk, 1, cols], aux(k), S_QK / (S_X * S_W), stg[:, qk, 0, cols]).then_inc(aux_free, 1)

            def s_max(sc, j, tiles):
                i, c = S_TILES[j]
                n, k = tiles.take()
                dve.wait_ge(aux_full, n + 1)
                out = mx[:, sc, c // 512, i:i + 1] if isinstance(sc, int) else mx[:, bass.ds(sc, 1), c // 512, i]
                v.tensor_reduce(out, aux(k, min(512, (i + 1) * P - c)), AX_X, ALU.max).then_inc(aux_free, 1)

            def in_order(b, g, tiles):
                dve.wait_ge(aux_free, tiles.first + tiles.n)
                mc = mxc[:, :].rearrange("p (h i) -> p h i", h=HPC)
                v.tensor_copy(mc[:, :, 0:HT], mx[:, :, 0, 0:HT])
                v.tensor_tensor(mc[:, :, HT:NT], mx[:, :, 0, HT:NT], mx[:, :, 1, HT:NT], ALU.max).then_inc(m_comb, 1)
                dve.wait_ge(m_comb, b * (NH // HPC) + g + 1)

            def maxima(b, g, tiles):
                n, k = tiles.take(2)
                dve.wait_ge(m_hi, b * (NH // HPC) + g + 1)
                v.scalar_tensor_tensor(out=mrow[0:HPC * NT, 1, :], in0=mrow[0:HPC * NT, 0, :], scalar=M_HI,
                                       in1=aux(k, P)[0:HPC * NT], op0=ALU.mult, op1=ALU.add).then_inc(aux_free, 2)

            def hi_copied(b, h, gi):
                by_act = NG - len(HI_BY_DVE)
                n = b * (NG * NH - LEAD * len(HI_BY_DVE))
                rank = gi + 1 - sum(g <= gi for g in HI_BY_DVE)
                return n + NG * (NH - LEAD) + (h - (NH - LEAD)) * by_act + rank

            def prob_lo(b, h, gi, beside_scores):
                w = group_blocks(gi)[1]
                if beside_scores:
                    n = b * (NG * NH - LEAD * len(HI_BY_DVE)) + h * NG + gi
                    dve.wait_ge(ph_done, n + 1)
                else:
                    dve.wait_ge(ph_done, hi_copied(b, h, gi))
                v.tensor_tensor(phl[:, gi % 3, 1, 0:w], p32[:, gi % 3, 0:w], phl[:, gi % 3, 0, 0:w],
                                ALU.subtract).then_inc(pl_done, 1)

            def prob_both(n, gi, k):
                w = group_blocks(gi)[1]
                dve.wait_ge(exp_done, n + 1)
                dve.wait_ge(pv_done, n - 2)
                v.tensor_copy(phl[:, gi % 3, 0, 0:w], p32[:, gi % 3, 0:w]).then_inc(ph_dve, 1)
                dve.wait_ge(ph_dve, k + 1)
                v.tensor_tensor(phl[:, gi % 3, 1, 0:w], p32[:, gi % 3, 0:w], phl[:, gi % 3, 0, 0:w],
                                ALU.subtract).then_inc(pl_done, 1)

            def recip(b, h, half):
                n = 2 * (b * NH + h) + half
                dve.wait_ge(o_copied, n + 1)
                v.reciprocal(orec[:, half, :, :], osb[:, half, :, DH:DH + 1]).then_inc(o_recip, 1)

            def step(b, h, tiles, s=None, sc=None, a={}, ln=None, m=None):
                fresh = isinstance(h, int) and h == 0
                if m is not None:
                    in_order(b, m, tiles)
                for gi in range(NG):
                    n = NG * (b * NH + h) + gi
                    if s is not None:
                        s_max(sc, 2 * gi, tiles)
                    if s is None and gi - 2 in HI_BY_DVE:
                        k = len(HI_BY_DVE) * (b * (LEAD) + (h - (NH - LEAD))) + HI_BY_DVE.index(gi - 2)
                        prob_both(n - 2, gi - 2, k)
                    elif not (fresh and gi < 2):
                        prob_lo(b, h if gi >= 2 else h - 1, (gi - 2) % NG,
                                s is not None or (gi < 2 and isinstance(h, int)))
                    if s is not None:
                        s_max(sc, 2 * gi + 1, tiles)
                    if gi == 3 and not fresh:
                        recip(b, h - 1, 1)
                    if gi == 5:
                        recip(b, h, 0)
                    if gi in a:
                        a_part(b, *a[gi], tiles)
                    if ln is not None and gi == 0:
                        ln_stats((b + 1) * NT + ln)
                    if m is not None and gi == 2:
                        maxima(b, m, tiles)
                    if ln is not None and gi == 5:
                        ln_lo((b + 1) * NT + ln, ln, tiles)

            def beside(b, items, tiles):
                for kind, *what in items:
                    if kind == "ln":
                        ln_lo(b * NT + NT - 1, NT - 1, tiles)
                    elif kind == "v":
                        v_part(b * NT + what[0], what[0], tiles)
                    elif kind == "a":
                        a_part(b, *what, tiles)
                    elif kind == "s":
                        s_max(what[0] % HPC, what[1], tiles)
                    elif kind == "in order":
                        in_order(b, 0, tiles)
                    elif kind == "rows":
                        maxima(b, 0, tiles)

            def after(b, post, more):
                tiles = tiles_after(b, more)
                if post:
                    prob_lo(b, NH - 1, NG - 2, False)
                    prob_lo(b, NH - 1, NG - 1, False)
                    recip(b, NH - 1, 1)
                if more:
                    ln_stats((b + 1) * NT + NT - 1)
                r_steps = [0]
                best_groups, best_experts, to_slots = routing(dve, b, r_steps)
                for s in range(TURNS):
                    u = b * NT + s - 2
                    if post and 2 <= s < NT + 2:
                        dve.wait_ge(x2_hi, u + 1)
                        rest_of(x2T[:, s % 2, 1, :], bank(TX), S_X, x2T[:, s % 2, 0, :]).then_inc(x2_lo, 1)
                    if post and s < NT:
                        dve.wait_ge(ot_hi, b * NT + s + 1)
                        v.tensor_tensor(oT[:, s % 2, 1, :], bank(TO), oT[:, s % 2, 0, :], ALU.subtract).then_inc(ot_lo, 1)
                    if post and 1 <= s < NT + 1:
                        t, k = s - 1, 2 * s - 1
                        dve.wait_ge(a_norm, b * NT + t + 1)
                        dve.wait_ge(xres_in[t % 2], (b * (NT // 2) + t // 2) * 16 + 16)
                        v.tensor_tensor(x1[:, t % 2, :], x1[:, t % 2, :], xn[:, t % 2, :], ALU.add).then_inc(x1_ready, 1)
                        dve.wait_ge(x1_ready, b * NT + t + 1)
                        v.bn_stats(st2[:, k % 4, :], x1[:, t % 2, :]).then_inc(p_st, 1)
                        hold("dve", dve, p_st, b * (2 * NT) + k + 1)
                        v.bn_aggr(mv2[:, k % 4, :], st2[:, k % 4, :]).then_inc(p_stat, 1)
                    if post and s == HT + 2:
                        best_groups(0)
                    if post and s == HT + 3:
                        best_experts(0)
                    if post and s == HT + 4:
                        to_slots(0, tiles)
                    if post and s == TURNS - 1:
                        best_groups(1)
                        best_experts(1)
                    if more:
                        beside(b + 1, BESIDE[s][0], tiles)
                    if post and 2 <= s < NT + 2:
                        dve.wait_ge(ff_exp, u + 1)
                        v.tensor_scalar(gex, gex, 1.0, None, ALU.add).then_inc(h_step, 1)
                        dve.wait_ge(h_step, u * 4 + 1)
                        v.reciprocal(grc, gex[:, 0:FF]).then_inc(h_step, 1)
                        v.reciprocal(sc_t[:, s - 2, :], gex[:, FF:FF + E]).then_inc(h_step, 1)
                        if s >= 3:
                            dve.wait_ge(th_psum, u)
                        dve.wait_ge(h_step, u * 4 + 3)
                        v.tensor_tensor(hid, bank(FU, FF), grc, ALU.mult).then_inc(h_step, 1)
                        dve.wait_ge(h_step, u * 4 + 4)
                        v.tensor_tensor(hid, bank(FU, FF, FF + E), hid, ALU.mult).then_inc(h_ready, 1)
                    if post and s < NT:
                        k, c = 2 * s, (2 * s) % 4
                        dve.wait_ge(a_psum, b * NT + s + 1)
                        v.bn_stats(st2[:, c, :], bank(AO)).then_inc(p_st, 1)
                        hold("dve", dve, p_st, b * (2 * NT) + k + 1)
                        v.bn_aggr(mv2[:, c, :], st2[:, c, :]).then_inc(p_stat, 1)
                    if more:
                        beside(b + 1, BESIDE[s][1], tiles)
                    if more:
                        beside(b + 1, BESIDE[s][2], tiles)
                    if post and 2 <= s < NT + 2:
                        dve.wait_ge(ht_hi, u * 2 + 2)
                        rest_of(hT[:, 1, 0, :], bank(TH, P), H_SCALE, hT[:, 0, 0, :]).then_inc(ht_lo, 1)
                        rest_of(hT[0:FR, 1, 1, :], bank(TH, P, P)[0:FR], H_SCALE, hT[0:FR, 0, 1, :]).then_inc(ht_lo, 1)
                if post:
                    to_slots(1, tiles)
                    assert r_steps[0] == RS, r_steps

            tiles = Tiles(0)
            for t in range(NT - 1):
                ln_stats(t)
                if 1 <= t <= len(SPLITS):
                    src, dst = SPLITS[t - 1]
                    dve.wait_ge(s_whi, t)
                    v.scalar_tensor_tensor(out=dst[:, 1], in0=src, scalar=S_W, in1=dst[:, 0], op0=ALU.mult,
                                           op1=ALU.subtract).then_inc(s_wlo, 1)
                ln_lo(t, t, tiles)
            after(-1, False, True)
            with dve.Fori(0, NB - 1) as b:
                loop_over_heads(dve, b, step, lambda b, g: None, True)
                after(b, True, True)
            loop_over_heads(dve, NB - 1, step, lambda b, g: None, False)
            after(NB - 1, True, False)
            experts_dve(dve)

        @block.tensor
        def _(pe):
            def mm(o, l, r, start, stop, **kw):
                return nc.tensor.matmul(o, l, r, start=start, stop=stop, **kw)

            def split3(o, lhs, rhs, parts=((0, P),) * C):
                k = 0
                for c in range(len(parts)):
                    for l, r in ((0, 0), (0, 1), (1, 0)):
                        ins = mm(o, lhs(l, c), rhs(r, c), k == 0, k == 3 * len(parts) - 1)
                        k += 1
                return ins

            def transposes(o, src):
                for c in range(C):
                    ins = nc.tensor.transpose(o[:, c * P:(c + 1) * P], src[:, c * P:(c + 1) * P], ident[:, :])
                return ins

            def free_aux(n):
                if not (isinstance(n, int) and n < 2):
                    pe.wait_ge(aux_free, n - 1)

            def ln_turn(n, tiles):
                m, k = tiles.take(2)
                pe.wait_ge(xl_ready, n + 2)
                free_aux(m)
                transposes(aux(k), xl).then_inc(aux_full, 2)

            def v_part(t, tiles):
                n, k = tiles.take()
                free_aux(n)
                split3(aux(k), lambda l, c: xT[:, l, c, t * P:(t + 1) * P],
                       lambda l, c: wqkv[:, l, c, 2 * D:3 * D]).then_inc(aux_full, 1)

            def a_part(g, qk, half, tiles):
                n, k = tiles.take()
                free_aux(n)
                split3(aux(k), lambda l, c: wqkv[:, l, c, bass.ds(g * P + qk * D, P)],
                       lambda l, c: xT[:, l, c, half * HALF:(half + 1) * HALF]).then_inc(aux_full, 1)

            def s_part(s, j, tiles):
                i, c = S_TILES[j]
                n, k = tiles.take()
                free_aux(n)
                w = min(512, (i + 1) * P - c)
                last = c + w == (i + 1) * P
                ins = mm(aux(k, w), stq[0:3 * DH, s, i * P:(i + 1) * P], stk[0:3 * DH, s, c:c + w], True, True,
                         skip_group_check=True)
                if last:
                    ins = mm(aux(k)[:, w - P:w], ident_b[:, :], mask_qk[:, :], False, True, skip_group_check=True)
                ins.then_inc(aux_full, 1)

            def wait_stacks(b, g):
                for k in range(2):
                    pe.wait_ge(stacked[k], (b * (NH // HPC) + g + 1) * STK)

            def maxima(b, g, tiles):
                n, k = tiles.take(2)
                pe.wait_ge(m_comb, b * (NH // HPC) + g + 1)
                free_aux(n)
                nc.tensor.transpose(aux(k, P)[0:HPC * NT], mxc[:, :], ident[:, :]).then_inc(aux_full, 2)

            def wait_rows(b, g):
                hold("pe", pe, m_rows, (b * (NH // HPC) + g) * 32 + 32)

            def scores_t(b, h, gi, fresh):
                n = NG * (b * NH + h) + gi
                if not (fresh and gi < 2):
                    pe.wait_ge(exp_done, n - 1)
                blocks, _ = group_blocks(gi)
                base = 2 * (gi % 2) * 512
                for j, i0, w, col in blocks:
                    ins = mm(PS[:, base + col:base + col + w], stk[:, h, j * P:(j + 1) * P],
                             stq[:, h, i0 * P:i0 * P + w], col % 512 == 0, True, skip_group_check=True)
                    if j == i0:
                        ins = mm(PS[:, base + col:base + col + P], ident_b[:, :], mask_kq[:, :], False, True,
                                 skip_group_check=True)
                ins.then_inc(st_psum, 1)

            def values(b, h, gi, fresh=False):
                half = GROUPS[gi][0]
                blocks, _ = group_blocks(gi)
                pe.wait_ge(pl_done, NG * (b * NH + h) + gi + 1)
                first = gi == 0 or GROUPS[gi - 1][0] != half
                if first and not fresh:
                    pe.wait_ge(o_copied, 2 * (b * NH + h) - 1 + half)
                ob = o_bank(half)
                for j, i0, w, col in blocks:
                    for q in range(w // P):
                        for l in range(2):
                            ins = mm(ob[:, i0 + q - half * HT, :], phl[:, gi % 3, l, col + q * P:col + (q + 1) * P],
                                     vv[:, j, h, 0:2 * DH + 1], first and j == blocks[0][0] and q == 0 and l == 0, True,
                                     skip_group_check=True)
                ins.then_inc(pv_done, 1)

            def step(b, h, tiles, s=None, sc=None, a={}, ln=None, m=None):
                fresh = isinstance(h, int) and h == 0
                if m is not None and s is not None:
                    wait_stacks(b, m + 1)
                for gi in range(NG):
                    scores_t(b, h, gi, fresh)
                    if s is not None:
                        s_part(s, 2 * gi, tiles)
                    if gi >= 3:
                        values(b, h, gi - 3, fresh)
                    elif not fresh:
                        values(b, h - 1, gi + 3)
                    if s is not None:
                        s_part(s, 2 * gi + 1, tiles)
                    if gi in a:
                        a_part(*a[gi], tiles)
                    if m is not None and gi == 2:
                        maxima(b, m, tiles)
                    if ln is not None and gi == 5:
                        ln_turn((b + 1) * NT + ln, tiles)

            def beside(b, items, tiles):
                for kind, *what in items:
                    if kind == "ln":
                        ln_turn(b * NT + NT - 1, tiles)
                    elif kind == "v":
                        v_part(what[0], tiles)
                    elif kind == "a":
                        a_part(*what, tiles)
                    elif kind == "s":
                        if what[0] % HPC == 0 and what[1] == 0:
                            wait_stacks(b, what[0] // HPC)
                        s_part(*what, tiles)
                    elif kind == "rows":
                        maxima(b, 0, tiles)

            def after(b, post, more):
                tiles = tiles_after(b, more)
                if post:
                    for gi in range(3, NG):
                        values(b, NH - 1, gi)
                    pe.wait_ge(o_done, 2 * (b * NH + NH) + 2)
                for s in range(TURNS):
                    u, r = b * NT + s - 2, b * NT + s - 3
                    if post and 2 <= s < NT + 2:
                        pe.wait_ge(xn2_ready, u + 1)
                        if s >= 3:
                            pe.wait_ge(x2_lo, u)
                        transposes(bank(TX), xn[:, s % 2, :]).then_inc(tx_psum, 1)
                    if post and s < NT:
                        if s >= 1:
                            pe.wait_ge(ot_lo, b * NT + s)
                        transposes(bank(TO), o_sb[:, s, :]).then_inc(to_psum, 1)
                    if more:
                        beside(b + 1, BESIDE[s][0], tiles)
                    if post and 2 <= s < NT + 2:
                        pe.wait_ge(x2_lo, u + 1)
                        if s >= 3:
                            pe.wait_ge(h_ready, u)
                        split3(bank(FU, FW), lambda l, c: x2T[:, s % 2, l, c * P:(c + 1) * P],
                               lambda l, c: wff[:, l, c, :]).then_inc(ff_psum, 1)
                    if post and s < NT:
                        pe.wait_ge(ot_lo, b * NT + s + 1)
                        if s >= 1:
                            pe.wait_ge(a_norm, b * NT + s)
                        split3(bank(AO), lambda l, c: oT[:, s % 2, l, c * P:(c + 1) * P],
                               lambda l, c: wo[:, l, c, :]).then_inc(a_psum, 1)
                    if more:
                        beside(b + 1, BESIDE[s][1], tiles)
                    if post and s >= 3:
                        pe.wait_ge(ht_lo, r * 2 + 2)
                        if s >= 4:
                            pe.wait_ge(y_sb, r)
                        kp = (P, FR)
                        split3(bank(DN), lambda l, c: hT[0:kp[c], l, c, :], lambda l, c: wdn[0:kp[c], l, c, :],
                               kp).then_inc(dn_psum, 1)
                    if post and 2 <= s < NT + 2:
                        pe.wait_ge(h_ready, u + 1)
                        if s >= 3:
                            pe.wait_ge(ht_lo, u * 2)
                        nc.tensor.transpose(bank(TH, P), hid[:, 0:P], ident[:, :])
                        nc.tensor.transpose(bank(TH, P, P)[0:FR], hid[:, P:FF], ident[:, :]).then_inc(th_psum, 1)
                    if more:
                        beside(b + 1, BESIDE[s][2], tiles)
                    if post and s in (HT + 3, TURNS - 1):
                        hf = int(s == TURNS - 1)
                        n, k = tiles.take(2)
                        pe.wait_ge(r_carry, b * (2 * NT) + (hf + 1) * NT)
                        free_aux(n)
                        flat = lambda t: t[hf].rearrange("p t e -> p (t e)")
                        mm(aux(k, HT * E), earlier[:, :], flat(sel_b), True, False)
                        mm(aux(k, HT * E), ones_b[:, :], flat(before_b), False, True).then_inc(aux_full, 2)
                if more:
                    wait_rows(b + 1, 0)

            pe.wait_ge(s_const, N_CONST)
            tiles = Tiles(0)
            for t in range(NT - 1):
                ln_turn(t, tiles)
            pe.wait_ge(s_wlo, len(SPLITS))
            pe.wait_ge(s_vconst, V_CONST)
            after(-1, False, True)
            pe.wait_ge(s_rows, 3)
            with pe.Fori(0, NB - 1) as b:
                loop_over_heads(pe, b, step, wait_rows, True)
                after(b, True, True)
            loop_over_heads(pe, NB - 1, step, wait_rows, False)
            after(NB - 1, True, False)
            experts_pe(pe)


def kernel(**inputs):
    import numpy as _np
    import concourse.bacc as _bacc
    from concourse import mybir as _mybir
    from concourse.bass_utils import run_bass_kernel_spmd as _run

    nc = _bacc.Bacc("TRN2", target_bir_lowering=False, num_devices=1)
    pick = lambda name: _np.asarray(inputs[name])
    laid = {
        "x": pick("L0_attn_x"),
        "w_qkv_t": pick("L0_attn_w_project").T,
        "w_out_t": pick("L0_attn_w_out").T,
    }
    for name in ("gate_w", "bias", "w_gate", "w_up", "w_down", "ws_gate", "ws_up", "ws_down"):
        laid[name] = pick("L0_ffn_" + name)
    arrays, args = {}, []
    for name, a in laid.items():
        a = _np.ascontiguousarray(a)
        arrays[f"in_{name}_dram"] = a
        args.append(nc.dram_tensor(f"in_{name}_dram", a.shape, _mybir.dt.from_np(a.dtype), kind="ExternalInput").ap())
    shape = laid["x"].shape
    args.append(nc.dram_tensor("out_0_dram", shape, _mybir.dt.float32, kind="ExternalOutput").ap())
    sandwich_kernel(nc, *args)
    r = _run(nc, [arrays], core_ids=[0])
    return r.results[0]["out_0_dram"]
```
